# Optimizing a Trainium2 kernel written in Bass

```python
import numpy as np
import jax
import jax.numpy as jnp

def _softmax(x, axis=-1):
    return jax.nn.softmax(x, axis=axis)

def _gelu(x):
    return jax.nn.gelu(x, approximate=True)

def _silu(x):
    return jax.nn.silu(x)

def _sigmoid(x):
    return jax.nn.sigmoid(x)

def _layernorm(x, axis=-1, eps=1e-05):
    m = jnp.mean(x, axis=axis, keepdims=True)
    v = jnp.var(x, axis=axis, keepdims=True)
    return (x - m) / jnp.sqrt(v + eps)

def _scatter_add(tgt, idx, src, axis=0):
    return tgt.at[idx].add(src)

def _segment_sum(src, seg, n):
    return jax.ops.segment_sum(src, seg, n)
kernel_name = 'mk_seq_postln_d1_jaxref_r8_bdf2ec'

def setup_inputs(seed: int=0):
    np.random.seed(seed)
    _w = jnp.asarray

    def _L0_attn_setup():
        import jax, jax.numpy as jnp
        import numpy as np
        NUM_HEADS = 16
        FOCUS_FACTOR = 1.6
        HEAD_REGION = {0: 0, 1: 1, 2: 2}

        def _region_multipliers(seq_len: int, num_heads: int, factor: float) -> jnp.ndarray:
            first_end = max(1, seq_len // 3)
            second_end = max(first_end + 1, 2 * seq_len // 3)
            pos = jnp.arange(seq_len)
            regions = [pos < first_end, (pos >= first_end) & (pos < second_end), pos >= second_end]
            mult = np.ones((num_heads, seq_len), dtype=np.float32)
            mult = jnp.asarray(mult)
            for h, r in HEAD_REGION.items():
                if h < num_heads:
                    mult = mult.at[h].set(1.0 + (factor - 1.0) * regions[r].astype(jnp.float32))
            return mult
        key = jax.random.key(seed)
        k1, k2, k3, k4, k5 = jax.random.split(key, 5)
        B, S, D = (2, 256, 128)
        return {'hidden_states': jax.random.normal(k1, (B, S, D), dtype=jnp.float32), 'c_attn_w': jax.random.normal(k2, (D, 3 * D), dtype=jnp.float32) * 0.02, 'c_attn_b': jax.random.normal(k3, (3 * D,), dtype=jnp.float32) * 0.02, 'c_proj_w': jax.random.normal(k4, (D, D), dtype=jnp.float32) * 0.02, 'c_proj_b': jax.random.normal(k5, (D,), dtype=jnp.float32) * 0.02}
    _L0_attn_in = _L0_attn_setup()

    def _L0_ffn_setup():
        import jax, jax.numpy as jnp
        import numpy as np
        import math
        D_IN = 128
        FEATURES = (512, 512, 128)
        BATCH, SEQ = (8, 256)

        def _conn_dense(kernel_bool, x):
            w = jnp.where(kernel_bool, jnp.float32(1.0), jnp.float32(-1.0))
            return x @ w
        key = jax.random.key(seed)
        kx, kk0, kk1, kk2 = jax.random.split(key, 4)
        x = jax.random.normal(kx, (BATCH, SEQ, D_IN), dtype=jnp.float32)
        k0 = jax.random.randint(kk0, (2 * D_IN, FEATURES[0]), 0, 2).astype(jnp.bool_)
        k1 = jax.random.randint(kk1, (FEATURES[0], FEATURES[1]), 0, 2).astype(jnp.bool_)
        k2 = jax.random.randint(kk2, (FEATURES[1], FEATURES[2]), 0, 2).astype(jnp.bool_)
        s0 = jnp.asarray(1.0 / math.sqrt(2 * D_IN), dtype=jnp.float32)
        s1 = jnp.asarray(1.0 / math.sqrt(FEATURES[0]), dtype=jnp.float32)
        s2 = jnp.asarray(1.0 / math.sqrt(FEATURES[1]), dtype=jnp.float32)
        return {'x': x, 'k0': k0, 'k1': k1, 'k2': k2, 's0': s0, 's1': s1, 's2': s2}
    _L0_ffn_in = _L0_ffn_setup()
    _d = {'L0_attn_hidden_states': _L0_attn_in['hidden_states'], 'L0_attn_c_attn_w': _L0_attn_in['c_attn_w'], 'L0_attn_c_attn_b': _L0_attn_in['c_attn_b'], 'L0_attn_c_proj_w': _L0_attn_in['c_proj_w'], 'L0_attn_c_proj_b': _L0_attn_in['c_proj_b'], 'L0_ffn_k0': _L0_ffn_in['k0'], 'L0_ffn_k1': _L0_ffn_in['k1'], 'L0_ffn_k2': _L0_ffn_in['k2'], 'L0_ffn_s0': _L0_ffn_in['s0'], 'L0_ffn_s1': _L0_ffn_in['s1'], 'L0_ffn_s2': _L0_ffn_in['s2']}
    _x0 = _d['L0_attn_hidden_states']
    _d['L0_attn_hidden_states'] = jax.random.normal(jax.random.fold_in(jax.random.key(seed), 1), (16, 512, 128), dtype=_x0.dtype)
    del _x0
    return _d

def reference(L0_attn_hidden_states, L0_attn_c_attn_w, L0_attn_c_attn_b, L0_attn_c_proj_w, L0_attn_c_proj_b, L0_ffn_k0, L0_ffn_k1, L0_ffn_k2, L0_ffn_s0, L0_ffn_s1, L0_ffn_s2):

    def _L0_attn_ref(hidden_states, c_attn_w, c_attn_b, c_proj_w, c_proj_b):
        import jax, jax.numpy as jnp
        import numpy as np
        NUM_HEADS = 16
        FOCUS_FACTOR = 1.6
        HEAD_REGION = {0: 0, 1: 1, 2: 2}

        def _region_multipliers(seq_len: int, num_heads: int, factor: float) -> jnp.ndarray:
            first_end = max(1, seq_len // 3)
            second_end = max(first_end + 1, 2 * seq_len // 3)
            pos = jnp.arange(seq_len)
            regions = [pos < first_end, (pos >= first_end) & (pos < second_end), pos >= second_end]
            mult = np.ones((num_heads, seq_len), dtype=np.float32)
            mult = jnp.asarray(mult)
            for h, r in HEAD_REGION.items():
                if h < num_heads:
                    mult = mult.at[h].set(1.0 + (factor - 1.0) * regions[r].astype(jnp.float32))
            return mult
        B, S, D = hidden_states.shape
        H = NUM_HEADS
        hd = D // H
        qkv = hidden_states @ c_attn_w + c_attn_b
        q, k, v = jnp.split(qkv, 3, axis=-1)

        def _reshape(x):
            return x.reshape(B, S, H, hd).transpose(0, 2, 1, 3)
        q, k, v = (_reshape(q), _reshape(k), _reshape(v))
        scores = jnp.einsum('bhqd,bhkd->bhqk', q, k) / jnp.sqrt(jnp.float32(hd))
        causal = jnp.tril(jnp.ones((S, S), dtype=bool))
        mask_value = jnp.finfo(scores.dtype).min
        scores = jnp.where(causal[None, None], scores, mask_value)
        attn = jax.nn.softmax(scores, axis=-1)
        mult = _region_multipliers(S, H, FOCUS_FACTOR)
        scaled = attn * mult[None, :, None, :]
        scaled = scaled / jnp.sum(scaled, axis=-1, keepdims=True)
        div_heads = jnp.zeros((H,), dtype=bool)
        for h in HEAD_REGION:
            if h < H:
                div_heads = div_heads.at[h].set(True)
        attn = jnp.where(div_heads[None, :, None, None], scaled, attn)
        out = jnp.einsum('bhqk,bhkd->bhqd', attn, v)
        out = out.transpose(0, 2, 1, 3).reshape(B, S, D)
        out = out @ c_proj_w + c_proj_b
        return out

    def _L0_ffn_ref(x, k0, k1, k2, s0, s1, s2):
        import jax, jax.numpy as jnp
        import numpy as np
        import math
        D_IN = 128
        FEATURES = (512, 512, 128)
        BATCH, SEQ = (8, 256)

        def _conn_dense(kernel_bool, x):
            w = jnp.where(kernel_bool, jnp.float32(1.0), jnp.float32(-1.0))
            return x @ w
        h = jnp.concatenate([x, -x], axis=-1)
        h = s0 * _conn_dense(k0, h)
        h = jax.nn.relu(h) * 2
        h = s1 * _conn_dense(k1, h)
        h = jax.nn.relu(h) * 2
        h = s2 * _conn_dense(k2, h)
        return h
    x = L0_attn_hidden_states
    x = _layernorm(x + _L0_attn_ref(x, L0_attn_c_attn_w, L0_attn_c_attn_b, L0_attn_c_proj_w, L0_attn_c_proj_b), axis=-1)
    x = _layernorm(x + _L0_ffn_ref(x, L0_ffn_k0, L0_ffn_k1, L0_ffn_k2, L0_ffn_s0, L0_ffn_s1, L0_ffn_s2), axis=-1)
    return x

_drawn_inputs = setup_inputs


def setup_inputs(seed=0):
    import zlib

    import numpy as np

    out = dict(_drawn_inputs(seed))
    spreads = {}
    factors = {'L0_attn_c_attn_w': 8.0,
     'L0_attn_c_attn_b': 8.0,
     'L0_attn_c_proj_w': 7.335,
     'L0_attn_c_proj_b': 2.841}
    for name, (base, spread) in spreads.items():
        noise = np.random.default_rng([zlib.crc32(name.encode()), seed]).standard_normal(out[name].shape)
        drawn = base * np.exp(spread * noise) if base else spread * noise
        out[name] = jnp.asarray(drawn.astype(out[name].dtype))
    for name, factor in factors.items():
        out[name] = (out[name] * factor).astype(out[name].dtype)
    return out
```

```python
from contextlib import ExitStack

import concourse.bass as bass
from concourse import mybir

F32 = mybir.dt.float32
F32R = mybir.dt.float32r
BF16 = mybir.dt.bfloat16
ALU = mybir.AluOpType
ACT = mybir.ActivationFunctionType
AX = mybir.AxisListType

HEADS = 16
FOCUS = 1.6
EPS = 1e-5
NEG = -3.0e38

BANK_USES = (
    ("negmax1", 0), ("ffn1_0", -2), ("ffn1_1", -2), ("ffn1_2", -2), ("ffn1_3", -2), ("v", 1),
    ("tok_0", -1), ("tok_1", -1), ("tok_2", -1), ("tok_3", -1), ("ffn2", -2), ("xT", 2),
    ("negmax0", 1), ("attnT", -1), ("q", 2), ("k", 2), ("proj", -1),
    ("x1T", -1), ("ffn0_0", -1), ("ffn0_1", -1), ("ffn0_2", -1), ("ffn0_3", -1),
)


UNROLL = 2


class At:

    def __init__(self, c, reg=None):
        self.c, self.reg = c, reg

    def __add__(self, k):
        return At(self.c + k, self.reg)

    def times(self, per, plus=0):
        k = self.c * per + plus
        return k if self.reg is None else self.reg * (UNROLL * per) + k

    @property
    def parity(self):
        return self.c % 2


def block_kernel(nc, x, w_qkv, b_qkv, w_proj, b_proj, k0, k1, k2, s0, s1, s2, out):
    B, S, D = x.shape
    H, R = HEADS, D // HEADS
    P = 128
    T = S // P
    F = k0.shape[1]
    FT = F // P
    SCALE = float(R) ** -0.5
    G = 4
    STEPS = 10
    HALF = H // 2
    QK_ROWS, MAX_ROW = 96, 96
    ALL_ROWS = MAX_ROW + 3
    FIRST, LAST = -2, B + 1
    LOOP = (3, B - 3)
    assert (D, H, T, FT, R) == (128, 16, 4, 4, 8) and (LOOP[1] - LOOP[0]) % UNROLL == 0

    def live(b):
        return b.reg is not None or 0 <= b.c < B

    USES = len(BANK_USES)
    used_before = {FIRST: 0}
    for n in range(FIRST, LAST + 1):
        used_before[n + 1] = used_before[n] + sum(0 <= n + d < B for _, d in BANK_USES)
    assert used_before[LOOP[1]] - used_before[LOOP[0]] == USES * (LOOP[1] - LOOP[0]) and USES % 2 == 0

    def use(n, what):
        before = [d for w, d in BANK_USES[:[w for w, _ in BANK_USES].index(what)]]
        if n.reg is None:
            i = used_before[n.c] + sum(0 <= n.c + d < B for d in before)
            return i % 2, i // 2 + 1
        i = used_before[LOOP[0]] + USES * (n.c - LOOP[0]) + len(before)
        return i % 2, n.reg * (UNROLL * USES // 2) + (i // 2 + 1)

    def use_of(b, what):
        return use(b + -dict(BANK_USES)[what], what)

    with ExitStack() as ctx:
        def sb(name, shape, dt=F32):
            return ctx.enter_context(nc.sbuf_tensor(name, shape, dt))

        def sem(name):
            return ctx.enter_context(nc.semaphore(name))

        score_ps = ctx.enter_context(nc.psum_tensor("score_ps", [P, 2, S], F32))
        max_ps = ctx.enter_context(nc.psum_tensor("max_ps", [P, 2, S], F32))
        av_ps = ctx.enter_context(nc.psum_tensor("av_ps", [P, 2, S], F32))
        bank_ps = ctx.enter_context(nc.psum_tensor("bank_ps", [P, 2, S], F32))

        ident = sb("ident", [P, P])
        ident_bf = sb("ident_bf", [P, P], BF16)
        future_bf = sb("future_bf", [P, P], BF16)
        mult = sb("mult", [P, T, 3])
        minus_half = sb("minus_half", [P, T])
        one = sb("one", [1, P])
        wc = sb("wc", [P, 3 * D])
        wqk = sb("wqk", [P, 2, P])
        wp = sb("wp", [P, D])
        bqk_row = sb("bqk_row", [1, 3 * D])
        bqk_perm = sb("bqk_perm", [1, 2, P])
        bqk = sb("bqk", [P, 2])
        bv = sb("bv", [P, D])
        bp = sb("bp", [P, D])
        scales = sb("scales", [P, 3])
        scales2 = sb("scales2", [P, 3])
        w0 = sb("w0", [P, F], F32R)
        w1 = sb("w1", [P, FT, F], F32R)
        w2 = sb("w2", [P, FT, D], F32R)

        stack = [sb(f"stack{i}", [P, H, 2, S], BF16) for i in range(2)]
        x_in = sb("x_in", [P, T, D])
        x_res = sb("x_res", [P, T, D])
        xT = sb("xT", [P, S])
        qk = sb("qk", [P, 2, S])
        parts = sb("parts", [P, 6, S], BF16)
        vaug = [sb(f"vaug{i}", [P, T, H, R + 1]) for i in range(2)]
        negmax = sb("negmax", [P, 2, T, HALF])
        negmax_rest = sb("negmax_rest", [P, 2, T, HALF])
        negmax_parts = sb("negmax_parts", [P, 2, T, 3, HALF], BF16)
        negmaxT = sb("negmaxT", [3 * HALF, 2, S], BF16)
        e = [sb(f"e{i}", [P, STEPS, S]) for i in range(2)]
        avT = sb("avT", [P, G, S])
        recip = sb("recip", [P, 2, H])
        attn = sb("attn", [P, T, D])
        attnT = sb("attnT", [P, S])
        res1 = sb("res1", [P, T, D])
        x1 = sb("x1", [P, T, D])
        stats = sb("stats", [P, 2, T, 6])
        moments = sb("moments", [P, 2, T, 2])
        var_eps = sb("var_eps", [P, 2, T])
        rstd = sb("rstd", [P, 2, T])
        full = sb("full", [P, 2, S])
        x1_hi = sb("x1_hi", [P, S], F32R)
        x1_lo = sb("x1_lo", [P, S], F32R)
        h_hi = [sb(f"h{i}_hi", [P, FT, S], F32R) for i in range(2)]
        h_lo = [sb(f"h{i}_lo", [P, FT, S], F32R) for i in range(2)]
        res2 = sb("res2", [P, T, D])

        raw0 = e[0][:, 0:2, :].rearrange("p a s -> p (a s)").bitcast(mybir.dt.uint8)[:, 0:2 * F]
        raw1 = e[0][:, 2:4, :].rearrange("p a s -> p (a s)").bitcast(mybir.dt.uint8)[:, 0:FT * F]
        raw2 = e[0][:, 4:5, :].rearrange("p a s -> p (a s)").bitcast(mybir.dt.uint8)[:, 0:FT * D]
        w0_half = e[0][:, 5, :]

        w_loaded = sem("w_loaded")
        ffn_loaded = sem("ffn_loaded")
        consts_step = sem("consts_step")
        consts_ready = sem("consts_ready")
        stack_cleared = sem("stack_cleared")
        setup_step = sem("setup_step")
        bias_row = sem("bias_row")
        x_loaded = sem("x_loaded")
        xres_loaded = sem("xres_loaded")
        xres_biased = sem("xres_biased")
        bank_full = [sem(f"bank{i}_full") for i in range(2)]
        bank_free = [sem(f"bank{i}_free") for i in range(2)]
        split_step = sem("split_step")
        stacked = [sem(f"stacked{i}") for i in range(2)]
        v_added = sem("v_added")
        v_ready = sem("v_ready")
        max_scored = sem("max_scored")
        max_taken = sem("max_taken")
        negmax_step = sem("negmax_step")
        negmax_in = [sem(f"negmax_in{i}") for i in range(2)]
        scored = sem("scored")
        exped = sem("exped")
        masked = sem("masked")
        summed = sem("summed")
        av_out = sem("av_out")
        recip_ready = sem("recip_ready")
        ln_step = [sem(f"ln{i + 1}_step") for i in range(2)]
        rstd_ready = [sem(f"rstd{i + 1}_ready") for i in range(2)]
        hi_ready = sem("hi_ready")
        split_ready = sem("split_ready")
        stored = sem("stored")

        x_tok = x.rearrange("b (t p) d -> b p t d", p=P)
        out_tok = out.rearrange("b (t p) d -> b p t d", p=P)

        block = ctx.enter_context(nc.Block())

        def run(eng, iteration):
            for n in range(FIRST, LOOP[0]):
                iteration(At(n))
            with eng.Fori(0, (LOOP[1] - LOOP[0]) // UNROLL) as i:
                for u in range(UNROLL):
                    iteration(At(LOOP[0] + u, i))
            for n in range(LOOP[1], LAST + 1):
                iteration(At(n))

        def wait_full(eng, u):
            eng.wait_ge(bank_full[u[0]], u[1])

        def wait_free(eng, u):
            eng.wait_ge(bank_free[u[0]], u[1])

        def apart(eng):
            eng.nop(nofuse=True)

        def full_slot(b, k):
            return (b.c * 9 + k) % 2

        @block.sync
        def _(sp):
            sp.dma_start(x_in[:], x_tok[0]).then_inc(x_loaded, 16)
            sp.dma_start(wc[:], w_qkv).then_inc(w_loaded, 16)
            sp.dma_start(bqk_row[:], b_qkv.rearrange("(a n) -> a n", a=1)).then_inc(w_loaded, 16)
            sp.dma_start(bv[:], b_qkv[2 * D:3 * D].partition_broadcast(P)).then_inc(w_loaded, 16)
            sp.dma_start(bp[:], b_proj.partition_broadcast(P)).then_inc(w_loaded, 16)
            sp.dma_start(wp[:], w_proj).then_inc(w_loaded, 16)
            sp.dma_start(raw0.rearrange("p (a n) -> p a n", a=2),
                         k0.rearrange("(a p) n -> p a n", p=P)).then_inc(ffn_loaded, 16)
            sp.dma_start(raw1.rearrange("p (a n) -> p a n", a=FT),
                         k1.rearrange("(a p) n -> p a n", p=P)).then_inc(ffn_loaded, 16)
            sp.dma_start(raw2.rearrange("p (a n) -> p a n", a=FT),
                         k2.rearrange("(a p) n -> p a n", p=P)).then_inc(ffn_loaded, 16)
            for i, s in enumerate((s0, s1, s2)):
                sp.dma_start(scales[:, i:i + 1], s.partition_broadcast(P)).then_inc(ffn_loaded, 16)

            def stack_half(b, half):
                for a in range(3):
                    for c in range(3):
                        row = R * (3 * a + c)
                        src = parts[64 * half:64 * half + 64, c:3 + a + 1:3 + a - c, :]
                        sp.dma_start(stack[b.parity][row:row + R, HALF * half:HALF * half + HALF, :, :],
                                     src).then_inc(stacked[half], 16)

            def negmax_rows(b, half):
                wait_free(sp, use_of(b, f"negmax{half}"))
                sp.dma_start(stack[b.parity][MAX_ROW:ALL_ROWS, HALF * half:HALF * half + HALF, 0, :],
                             negmaxT[:, half, :]).then_inc(negmax_in[half], 16)

            def iteration(n):
                b = n + 2
                if live(b) and not (b.reg is None and b.c == 0):
                    wait_full(sp, use_of(b + -1, "xT"))
                    sp.dma_start(x_in[:], x_tok[b.times(1)]).then_inc(x_loaded, 16)
                b = n + -1
                if live(b):
                    if b.c > 0 or b.reg is not None:
                        wait_free(sp, use_of(b + -1, "proj"))
                    sp.dma_start(x_res[:], x_tok[b.times(1)]).then_inc(xres_loaded, 16)
                if live(n):
                    negmax_rows(n, 1)
                b = n + -2
                if live(b):
                    sp.wait_ge(ln_step[1], b.times(4, 4))
                    sp.dma_start(out_tok[b.times(1)], res2[:]).then_inc(stored, 16)
                if live(n + 1):
                    negmax_rows(n + 1, 0)
                b = n + 2
                if live(b):
                    sp.wait_ge(split_step, b.times(4, 4))
                    apart(sp)
                    if live(n):
                        sp.wait_ge(scored, n.times(G * STEPS, 2 * STEPS))
                    else:
                        sp.wait_ge(stack_cleared, 4)
                    stack_half(b, 0)
                    if live(n):
                        sp.wait_ge(scored, n.times(G * STEPS, 4 * STEPS))
                    stack_half(b, 1)

            run(sp, iteration)
            sp.wait_ge(stored, 16 * B)

        @block.gpsimd
        def _(pool):
            step = 0
            for t, v in ((ident, 0.0), (ident_bf, 0.0), (future_bf, 0.0), (mult, FOCUS)):
                nc.gpsimd.memset(t[:], v).then_inc(consts_step, 1)
                step += 1
            nc.gpsimd.memset(minus_half[:], -0.5).then_inc(consts_step, 1)
            nc.gpsimd.memset(one[:], 1.0).then_inc(consts_step, 1)
            step += 2
            pool.wait_ge(consts_step, step)
            for t in (ident, ident_bf):
                nc.gpsimd.affine_select(out=t[:], in_=t[:], compare_op=ALU.not_equal, fill=1.0, base=0,
                                        pattern=[[-1, P]], channel_multiplier=1).then_inc(consts_step, 1)
            nc.gpsimd.affine_select(out=future_bf[:], in_=future_bf[:], compare_op=ALU.is_ge, fill=NEG, base=0,
                                    pattern=[[1, P]], channel_multiplier=-1).then_inc(consts_step, 1)
            first_end = max(1, S // 3)
            second_end = max(first_end + 1, 2 * S // 3)
            step += 3
            for h, base, sign in ((0, first_end - 1, -1), (1, -first_end, 1), (2, -second_end, 1),
                                  (1, second_end - 1, -1)):
                pool.wait_ge(consts_step, step)
                nc.gpsimd.affine_select(out=mult[:, :, h:h + 1], in_=mult[:, :, h:h + 1], compare_op=ALU.is_ge,
                                        fill=1.0, base=base, pattern=[[sign * P, T], [0, 1]],
                                        channel_multiplier=sign).then_inc(consts_step, 1)
                step += 1
            pool.wait_ge(consts_step, step)
            nc.gpsimd.memset(recip[:], 1.0).then_inc(consts_ready, 1)
            pool.wait_ge(consts_ready, 1)
            for i in range(2):
                pool.wait_ge(stack_cleared, 2 + i)
                nc.gpsimd.memset(stack[i][MAX_ROW:P, :, 1, :], 1.0).then_inc(stack_cleared, 1)

            def split(b, k):
                hi, mid, lo = (parts[:, i:i + 4:3, :] for i in range(3))
                if k == 0:
                    if b.c > 0 or b.reg is not None:
                        for half in range(2):
                            pool.wait_ge(stacked[half], b.times(9 * 16))
                    wait_free(pool, use_of(b, "q"))
                    wait_free(pool, use_of(b, "k"))
                else:
                    pool.wait_ge(split_step, b.times(4, k))
                if k % 2 == 0:
                    apart(pool)
                if k == 0:
                    ins = nc.gpsimd.tensor_copy(hi, qk[:])
                elif k == 1:
                    ins = nc.gpsimd.tensor_tensor(qk[:], qk[:], hi, ALU.subtract)
                elif k == 2:
                    ins = nc.gpsimd.tensor_copy(mid, qk[:])
                else:
                    ins = nc.gpsimd.tensor_tensor(lo, qk[:], mid, ALU.subtract)
                ins.then_inc(split_step, 1)

            def mask(n, g, k):
                buf = e[g % 2]
                if k == 0:
                    after, blocks = 4, (buf[:, 0:4, 0:P],)
                elif k == 1:
                    after, blocks = 8, (buf[:, 4:8, 0:P], buf[:, 4:8, 3 * P:S])
                else:
                    halves = buf[:, 8:10, :].rearrange("p h (a c) -> p (h a) c", c=2 * P)
                    after, blocks = 10, (halves[:, :, 0:P],)
                pool.wait_ge(exped, n.times(G * STEPS, STEPS * g + after))
                apart(pool)
                for ap in blocks:
                    last = nc.gpsimd.affine_select(out=ap, in_=ap, compare_op=ALU.is_ge, fill=0.0, base=0,
                                                   pattern=[[0, 4], [1, P]], channel_multiplier=-1)
                last.then_inc(masked, 1)

            def low_part(b, m):
                k = 5 + m
                pool.wait_ge(hi_ready, b.times(9, k + 1))
                nc.gpsimd.tensor_tensor(h_lo[1][:, m, :], full[:, full_slot(b, k), :],
                                        h_hi[1][:, m, :].bitcast(F32), ALU.subtract).then_inc(split_ready, 1)

            def rstd_of(b, i):
                pool.wait_ge(ln_step[i], b.times(4, 3))
                nc.gpsimd.tensor_tensor(rstd[:, i, :], var_eps[:, i, :], minus_half[:],
                                        ALU.pow).then_inc(rstd_ready[i], 1)

            def iteration(n):
                for g in range(G):
                    if g == 0 and live(n + -2):
                        low_part(n + -2, 0)
                        low_part(n + -2, 1)
                    if live(n):
                        mask(n, g, 0)
                    if g == 0 and live(n + -2):
                        low_part(n + -2, 2)
                        low_part(n + -2, 3)
                    if g == 1 and live(n + -1):
                        b = n + -1
                        pool.wait_ge(xres_loaded, b.times(16, 16))
                        nc.gpsimd.tensor_tensor(x_res[:], x_res[:], bp[:].unsqueeze(1).broadcast_to([P, T, D]),
                                                ALU.add).then_inc(xres_biased, 1)
                    if g == 3 and live(n + 2):
                        split(n + 2, 0)
                        split(n + 2, 1)
                    if live(n):
                        mask(n, g, 1)
                    if g == 1 and live(n + -2):
                        rstd_of(n + -2, 1)
                    if g == 2 and live(n + -1):
                        rstd_of(n + -1, 0)
                    if live(n):
                        mask(n, g, 2)
                    if g == 3 and live(n + 2):
                        split(n + 2, 2)
                        split(n + 2, 3)

            pool.wait_ge(stack_cleared, 4)
            pool.wait_ge(w_loaded, 16 * 5)
            run(pool, iteration)

        @block.scalar
        def _(act):
            act.wait_ge(setup_step, 9)

            def take(u, out_ap, func, **kw):
                wait_full(act, u)
                nc.scalar.activation(out_ap, bank_ps[:, u[0], :], func, **kw).then_inc(bank_free[u[0]], 1)

            def exp(n, g, t):
                act.wait_ge(scored, n.times(G * STEPS, STEPS * g + t + 1))
                if t == 0 and not (n.reg is None and n.c * G + g < 2):
                    act.wait_ge(summed, n.times(G, g - 1))
                nc.scalar.activation(e[g % 2][:, t, :], score_ps[:, t % 2, :], ACT.Exp,
                                     scale=SCALE).then_inc(exped, 1)

            def sums_out(b, g):
                act.wait_ge(summed, b.times(G, g + 1))
                if g == 0 and (b.reg is not None or b.c > 0):
                    wait_full(act, use_of(b + -1, "tok_3"))
                nc.scalar.activation(avT[:, g, :], av_ps[:, g % 2, :], ACT.Copy).then_inc(av_out, 1)

            def activation_out(b, k, what, func, **kw):
                if b.reg is not None or b.c * 9 + k >= 2:
                    act.wait_ge(split_ready, b.times(9, k - 1))
                take(use_of(b, what), full[:, full_slot(b, k), :], func, **kw)

            def iteration(n):
                for g in range(G):
                    for t in range(STEPS):
                        if live(n):
                            exp(n, g, t)
                        if t == 5:
                            if g == 0 and live(n + -1):
                                sums_out(n + -1, 3)
                            if g > 0 and live(n):
                                sums_out(n, g - 1)
                        if g == 0 and t in (1, 3, 5, 7) and live(n + -2):
                            m = t // 2
                            activation_out(n + -2, 5 + m, f"ffn1_{m}", ACT.Relu, scale=scales2[:, 1:2])
                        if g == 1 and t == 7 and live(n + 2):
                            if live(n + 1):
                                wait_full(act, use_of(n + 1, "v"))
                            take(use_of(n + 2, "xT"), xT[:], ACT.Copy)
                        if g == 2 and t == 2 and live(n + -1):
                            take(use_of(n + -1, "attnT"), attnT[:], ACT.Copy)
                        if g == 2 and t in (4, 5) and live(n + 2):
                            b, i = n + 2, t - 4
                            if i == 0 and (b.reg is not None or b.c > 0):
                                act.wait_ge(split_step, b.times(4))
                            take(use_of(b, "qk"[i]), qk[:, i, :], ACT.Identity, bias=bqk[:, i:i + 1])
                        if g == 3 and t == 1 and live(n + -1):
                            activation_out(n + -1, 0, "x1T", ACT.Copy)
                        if g == 3 and 3 <= t < 7 and live(n + -1):
                            activation_out(n + -1, 1 + t - 3, f"ffn0_{t - 3}", ACT.Relu, scale=scales[:, 0:1])

            run(act, iteration)

        @block.vector
        def _(dve):
            for i in range(2):
                nc.vector.memset(stack[i][64:P].rearrange("p h a s -> p (h a s)").bitcast(F32),
                                 0.0).then_inc(stack_cleared, 1)
            nc.vector.memset(av_ps[:], 0.0).then_inc(setup_step, 1)
            for i in range(2):
                nc.vector.memset(vaug[i][:, :, :, R:R + 1], 1.0).then_inc(setup_step, 1)
            dve.wait_ge(w_loaded, 16 * 5)
            for i in range(2):
                for half in range(2):
                    hs = slice(D * i + 64 * half, D * i + 64 * half + 64)
                    ws = wc[:, hs].rearrange("p (h r) -> p r h", r=R)
                    bs = bqk_row[:, hs].rearrange("p (h r) -> p r h", r=R)
                    nc.vector.tensor_copy(
                        wqk[:, i, 64 * half:64 * half + 64].rearrange("p (r h) -> p r h", r=R), ws)
                    last = nc.vector.tensor_copy(
                        bqk_perm[:, i, 64 * half:64 * half + 64].rearrange("p (r h) -> p r h", r=R), bs)
            last.then_inc(setup_step, 1)
            dve.wait_ge(consts_ready, 1)
            dve.wait_ge(setup_step, 4)
            for i in range(2):
                last = nc.vector.tensor_copy(vaug[i][:, :, 0:3, R:R + 1], mult[:].unsqueeze(3))
            last.then_inc(setup_step, 1)
            dve.wait_ge(bias_row, 1)
            nc.vector.tensor_copy(bqk[:], max_ps[:, 0, 0:2]).then_inc(setup_step, 1)
            dve.wait_ge(ffn_loaded, 16 * 6)
            nc.vector.tensor_scalar(scales2[:], scales[:], 2.0, None, ALU.mult).then_inc(setup_step, 1)
            nc.vector.tensor_scalar(w0_half, raw0[:, F:2 * F], -2.0, None, ALU.mult).then_inc(setup_step, 1)
            dve.wait_ge(setup_step, 8)
            nc.vector.scalar_tensor_tensor(w0[:], raw0[:, 0:F], 2.0, w0_half, ALU.mult, ALU.add)
            nc.vector.tensor_scalar(w1[:].rearrange("p a n -> p (a n)"), raw1, 2.0, -1.0, ALU.mult, ALU.add)
            nc.vector.tensor_scalar(w2[:].rearrange("p a n -> p (a n)"), raw2, 2.0, -1.0, ALU.mult,
                                    ALU.add).then_inc(setup_step, 1)

            def take_max(b, g, t):
                buf = max_ps[:, t % 2, :]
                half, h = g // 2, G * (g % 2)
                dve.wait_ge(max_scored, b.times(G * STEPS, STEPS * g + t + 1))
                if t < 4:
                    ins = nc.vector.reduce_max(negmax[:, half, 3, h + t:h + t + 1], buf, AX.X, negate=True)
                elif t < 8:
                    i = h + t - 4
                    nc.vector.reduce_max(negmax[:, half, 2, i:i + 1], buf[:, 0:3 * P], AX.X, negate=True)
                    ins = nc.vector.reduce_max(negmax[:, half, 0, i:i + 1], buf[:, 3 * P:S], AX.X, negate=True)
                else:
                    i = h + 2 * (t - 8)
                    ins = nc.vector.reduce_max(negmax[:, half, 1, i:i + 2],
                                               buf.rearrange("p (h k) -> p h k", h=2), AX.X, negate=True)
                ins.then_inc(max_taken, 1)

            def split_negmax(b, half):
                m, r = negmax[:, half], negmax_rest[:, half]
                hi, mid, lo = (negmax_parts[:, half, :, i, :] for i in range(3))
                dve.wait_ge(max_taken, b.times(G * STEPS, 2 * STEPS * (half + 1)))
                for k in range(4):
                    if k:
                        dve.wait_ge(negmax_step, b.times(8, 4 * half + k))
                    if k == 0:
                        ins = nc.vector.tensor_copy(hi, m)
                    elif k == 1:
                        ins = nc.vector.tensor_tensor(r, m, hi, ALU.subtract)
                    elif k == 2:
                        ins = nc.vector.tensor_copy(mid, r)
                    else:
                        ins = nc.vector.tensor_tensor(lo, r, mid, ALU.subtract)
                    ins.then_inc(negmax_step, 1)

            def take_negmaxT(b, half):
                u = use_of(b, f"negmax{half}")
                wait_full(dve, u)
                if b.reg is not None or b.c > 0:
                    dve.wait_ge(negmax_in[half], b.times(16))
                src = bank_ps[0:3 * HALF, u[0], :].bitcast(BF16)[:, 0:S]
                nc.vector.tensor_copy(negmaxT[:, half, :], src).then_inc(bank_free[u[0]], 1)

            def take_v(b):
                u = use_of(b, "v")
                wait_full(dve, u)
                va = vaug[b.parity]
                if b.reg is not None or b.c > 1:
                    dve.wait_ge(summed, b.times(G, -G))
                nc.vector.tensor_tensor(va[:, :, :, 0:R], bank_ps[:, u[0], :].rearrange("p (t h r) -> p t h r", t=T, r=R),
                                        bv[:].rearrange("p (h r) -> p h r", r=R).unsqueeze(1).broadcast_to([P, T, H, R]),
                                        ALU.add).then_inc(bank_free[u[0]], 1)
                wait_free(dve, u)
                nc.vector.tensor_tensor(va[:, :, 0:3, 0:R], va[:, :, 0:3, 0:R],
                                        mult[:].unsqueeze(3).broadcast_to([P, T, 3, R]), ALU.mult).then_inc(v_ready, 1)

            def normalise(b, t):
                u = use_of(b, f"tok_{t}")
                wait_full(dve, u)
                src = bank_ps[:, u[0], :].rearrange("p (h c) -> p h c", c=32)
                nc.vector.reciprocal(recip[:, t % 2, :].unsqueeze(2), src[:, :, R:R + 1]).then_inc(recip_ready, 1)
                dve.wait_ge(recip_ready, b.times(T, t + 1))
                nc.vector.tensor_tensor(attn[:, t, :].rearrange("p (h r) -> p h r", r=R), src[:, :, 0:R],
                                        recip[:, t % 2, :].unsqueeze(2).broadcast_to([P, H, R]),
                                        ALU.mult).then_inc(bank_free[u[0]], 1)

            def layernorm_stats(i, src, u):
                wait_free(dve, u)
                for t in range(T):
                    ins = nc.vector.bn_stats(stats[:, i, t, :], src[:, t, :])
                ins.then_inc(ln_step[i], 1)

            def layernorm_var(b, i):
                dve.wait_ge(ln_step[i], b.times(4, 1))
                apart(dve)
                for t in range(T):
                    ins = nc.vector.bn_aggr(moments[:, i, t, :], stats[:, i, t, :])
                ins.then_inc(ln_step[i], 1)
                dve.wait_ge(ln_step[i], b.times(4, 2))
                nc.vector.tensor_scalar(var_eps[:, i, :].unsqueeze(2), moments[:, i, :, 1:2], EPS, None,
                                        ALU.add).then_inc(ln_step[i], 1)

            def layernorm_out(b, i, src, dst):
                dve.wait_ge(rstd_ready[i], b.times(1, 1))
                for t in range(T):
                    ins = nc.vector.tensor_scalar(dst[:, t, :], src[:, t, :], moments[:, i, t, 0:1],
                                                  rstd[:, i, t:t + 1], ALU.subtract, ALU.mult)
                ins.then_inc(ln_step[i], 1)

            def high_part(b, k, hi, what):
                wait_free(dve, use_of(b, what))
                nc.vector.tensor_copy(hi, full[:, full_slot(b, k), :]).then_inc(hi_ready, 1)

            def low_part(b, k, hi, lo):
                dve.wait_ge(hi_ready, b.times(9, k + 1))
                nc.vector.tensor_tensor(lo, full[:, full_slot(b, k), :], hi.bitcast(F32),
                                        ALU.subtract).then_inc(split_ready, 1)

            def iteration(n):
                for g in range(G):
                    for t in range(STEPS):
                        if live(n + 1):
                            take_max(n + 1, g, t)
                        if g == 0:
                            if t == 1 and live(n):
                                take_negmaxT(n, 1)
                            if t in (1, 3, 5, 7) and live(n + -2):
                                m = t // 2
                                high_part(n + -2, 5 + m, h_hi[1][:, m, :], f"ffn1_{m}")
                            if t == 9 and live(n + 1):
                                take_v(n + 1)
                        if g == 1:
                            if t < 4 and live(n + -1):
                                normalise(n + -1, t)
                            if t == 6 and live(n + -2):
                                b = n + -2
                                u = use_of(b, "ffn2")
                                wait_full(dve, u)
                                if b.reg is not None or b.c > 0:
                                    dve.wait_ge(stored, b.times(16))
                                nc.vector.scalar_tensor_tensor(
                                    res2[:].rearrange("p t d -> p (t d)"), bank_ps[:, u[0], :], scales2[:, 2:3],
                                    x1[:].rearrange("p t d -> p (t d)"), ALU.mult, ALU.add).then_inc(bank_free[u[0]], 1)
                                layernorm_stats(1, res2, u)
                            if t == 7 and live(n + -2):
                                layernorm_var(n + -2, 1)
                            if t == 9 and live(n + -2):
                                layernorm_out(n + -2, 1, res2, res2)
                            if t == 9 and live(n + 1):
                                split_negmax(n + 1, 0)
                        if g == 2:
                            if t == 1 and live(n + 1):
                                take_negmaxT(n + 1, 0)
                            if t == 6 and live(n + -1):
                                b = n + -1
                                u = use_of(b, "proj")
                                wait_full(dve, u)
                                dve.wait_ge(xres_biased, b.times(1, 1))
                                nc.vector.tensor_tensor(res1[:].rearrange("p t d -> p (t d)"), bank_ps[:, u[0], :],
                                                        x_res[:].rearrange("p t d -> p (t d)"),
                                                        ALU.add).then_inc(bank_free[u[0]], 1)
                                layernorm_stats(0, res1, u)
                            if t == 7 and live(n + -1):
                                layernorm_var(n + -1, 0)
                            if t == 9 and live(n + -1):
                                layernorm_out(n + -1, 0, res1, x1)
                        if g == 3:
                            if t == 1 and live(n + -1):
                                high_part(n + -1, 0, x1_hi[:], "x1T")
                                low_part(n + -1, 0, x1_hi[:], x1_lo[:])
                            if 3 <= t < 7 and live(n + -1):
                                m = t - 3
                                high_part(n + -1, 1 + m, h_hi[0][:, m, :], f"ffn0_{m}")
                                low_part(n + -1, 1 + m, h_hi[0][:, m, :], h_lo[0][:, m, :])
                            if t == 9 and live(n + 1):
                                split_negmax(n + 1, 1)

            run(dve, iteration)

        @block.tensor
        def _(pe):
            pe.wait_ge(setup_step, 4)
            pe.wait_ge(consts_ready, 1)
            for i in range(2):
                last = nc.tensor.matmul(max_ps[:, 0, i:i + 1], bqk_perm[0:1, i, :], one[0:1, 0:1],
                                        start=(i == 0), stop=True, skip_group_check=True)
            last.then_inc(bias_row, 1)
            pe.wait_ge(setup_step, 6)

            def claim(u):
                if not (isinstance(u[1], int) and u[1] == 1):
                    pe.wait_ge(bank_free[u[0]], u[1] + -1)
                return bank_ps[:, u[0], :]

            def transposes(u, sources, into=None):
                bank = claim(u)
                for i, src in enumerate(sources):
                    last = nc.tensor.transpose(bank[:, P * i:P * i + P], src, ident[:])
                last.then_inc(bank_full[u[0]], 1)

            def max_scores(b, g, t):
                st, out_ap = stack[b.parity], max_ps[:, t % 2, :]
                if t == 0 and g % 2 == 0:
                    pe.wait_ge(stacked[g // 2], b.times(9 * 16, 9 * 16))
                if not (b.reg is None and b.c == 0 and g == 0 and t < 2):
                    pe.wait_ge(max_taken, b.times(G * STEPS, STEPS * g + t - 1))

                def part(h, qt, col):
                    width = P * (qt + 1)
                    nc.tensor.matmul(out_ap[:, col:col + width], st[0:QK_ROWS, h, 0, P * qt:P * qt + P],
                                     st[0:QK_ROWS, h, 1, 0:width], start=True, stop=False)
                    return nc.tensor.matmul(out_ap[:, col + width - P:col + width], future_bf[:], ident_bf[:],
                                            start=False, stop=True)
                if t < 4:
                    last = part(G * g + t, 3, 0)
                elif t < 8:
                    part(G * g + t - 4, 2, 0)
                    last = part(G * g + t - 4, 0, 3 * P)
                else:
                    part(G * g + 2 * (t - 8), 1, 0)
                    last = part(G * g + 2 * (t - 8) + 1, 1, 2 * P)
                last.then_inc(max_scored, 1)

            def scores(n, g, t):
                st, out_ap = stack[n.parity], score_ps[:, t % 2, :]
                if t == 0 and g % 2 == 0:
                    pe.wait_ge(negmax_in[g // 2], n.times(16, 16))
                if not (n.reg is None and n.c == 0 and g == 0 and t < 2):
                    pe.wait_ge(exped, n.times(G * STEPS, STEPS * g + t - 1))

                def part(h, kt, col):
                    width = S - P * kt
                    return nc.tensor.matmul(out_ap[:, col:col + width], st[0:ALL_ROWS, h, 1, P * kt:P * kt + P],
                                            st[0:ALL_ROWS, h, 0, P * kt:S], start=True, stop=True)
                if t < 4:
                    last = part(G * g + t, 0, 0)
                elif t < 8:
                    part(G * g + t - 4, 1, 0)
                    last = part(G * g + t - 4, 3, 3 * P)
                else:
                    part(G * g + 2 * (t - 8), 2, 0)
                    last = part(G * g + 2 * (t - 8) + 1, 2, 2 * P)
                last.then_inc(scored, 1)

            def sums(b, g, kt, order):
                if order == 0:
                    pe.wait_ge(masked, b.times(3 * G, 3 * g + 1))
                    if g == 0:
                        pe.wait_ge(v_ready, b.times(1, 1))
                    if not (b.reg is None and b.c == 0 and g < 2):
                        pe.wait_ge(av_out, b.times(G, g - 1))
                elif order == 1:
                    pe.wait_ge(masked, b.times(3 * G, 3 * g + 2))
                elif order == 3:
                    pe.wait_ge(masked, b.times(3 * G, 3 * g + 3))
                for j in range(G):
                    if kt == 0:
                        src = e[g % 2][:, j, :]
                    elif kt == 1:
                        src = e[g % 2][:, 4 + j, 0:3 * P]
                    elif kt == 3:
                        src = e[g % 2][:, 4 + j, 3 * P:S]
                    else:
                        src = e[g % 2][:, 8 + j // 2, 2 * P * (j % 2):2 * P * (j % 2) + 2 * P]
                    last = nc.tensor.matmul(av_ps[32 * j:32 * j + R + 1, g % 2, P * kt:S],
                                            vaug[b.parity][:, kt, G * g + j, :], src,
                                            start=(order == 0), stop=(order == 3))
                if order == 3:
                    last.then_inc(summed, 1)

            def negmax_transposes(b, half):
                u = use_of(b, f"negmax{half}")
                pe.wait_ge(negmax_step, b.times(8, 4 * half + 4))
                bank = claim(u).bitcast(BF16)
                for qt in range(T):
                    last = nc.tensor.transpose(bank[0:3 * HALF, P * qt:P * qt + P],
                                               negmax_parts[:, half, qt].rearrange("p c h -> p (c h)"), ident_bf[:])
                last.then_inc(bank_full[u[0]], 1)

            def token_transposes(b, t):
                if t == 0:
                    pe.wait_ge(av_out, b.times(G, G))
                transposes(use_of(b, f"tok_{t}"), [avT[:, g, P * t:P * t + P] for g in range(G)])

            def ffn(b, what, pairs):
                u = use_of(b, what)
                bank = claim(u)
                for i, (w, hi, lo) in enumerate(pairs):
                    nc.tensor.matmul(bank, w, hi, start=(i == 0), stop=False)
                    last = nc.tensor.matmul(bank, w, lo, start=False, stop=(i == len(pairs) - 1))
                last.then_inc(bank_full[u[0]], 1)

            def fill(n, g, t):
                if g == 0:
                    if t == 1 and live(n):
                        negmax_transposes(n, 1)
                    if t in (1, 3, 5, 7) and live(n + -2):
                        m, b = t // 2, n + -2
                        if m == 0:
                            pe.wait_ge(split_ready, b.times(9, 5))
                        ffn(b, f"ffn1_{m}", [(w1[:, k, P * m:P * m + P], h_hi[0][:, k, :], h_lo[0][:, k, :])
                                             for k in range(FT)])
                    if t == 9 and live(n + 1):
                        u = use_of(n + 1, "v")
                        bank = claim(u)
                        wait_free(pe, use_of(n + 1, "xT"))
                        for kt in range(T):
                            last = nc.tensor.matmul(bank[:, P * kt:P * kt + P], xT[:, P * kt:P * kt + P],
                                                    wc[:, 2 * D:3 * D], start=True, stop=True)
                        last.then_inc(bank_full[u[0]], 1)
                if g == 1:
                    if t < 4 and live(n + -1):
                        token_transposes(n + -1, t)
                    if t == 6 and live(n + -2):
                        b = n + -2
                        u = use_of(b, "ffn2")
                        pe.wait_ge(split_ready, b.times(9, 9))
                        bank = claim(u)
                        for qt in range(T):
                            col = slice(P * qt, P * qt + P)
                            for k in range(FT):
                                nc.tensor.matmul(bank[:, col], h_hi[1][:, k, col], w2[:, k, :],
                                                 start=(k == 0), stop=False)
                                last = nc.tensor.matmul(bank[:, col], h_lo[1][:, k, col], w2[:, k, :],
                                                        start=False, stop=(k == FT - 1))
                        last.then_inc(bank_full[u[0]], 1)
                    if t == 7 and live(n + 2):
                        pe.wait_ge(x_loaded, (n + 2).times(16, 16))
                        transposes(use_of(n + 2, "xT"), [x_in[:, i, :] for i in range(T)])
                if g == 2:
                    if t == 1 and live(n + 1):
                        negmax_transposes(n + 1, 0)
                    if t == 2 and live(n + -1):
                        wait_free(pe, use_of(n + -1, "tok_3"))
                        transposes(use_of(n + -1, "attnT"), [attn[:, i, :] for i in range(T)])
                    if t in (4, 5) and live(n + 2):
                        b, i = n + 2, t - 4
                        u = use_of(b, "qk"[i])
                        bank = claim(u)
                        wait_free(pe, use_of(b, "xT"))
                        nc.tensor.matmul(bank, wqk[:, i, :], xT[:], start=True, stop=True).then_inc(bank_full[u[0]], 1)
                    if t == 6 and live(n + -1):
                        u = use_of(n + -1, "proj")
                        bank = claim(u)
                        wait_free(pe, use_of(n + -1, "attnT"))
                        for i in range(T):
                            last = nc.tensor.matmul(bank[:, P * i:P * i + P], attnT[:, P * i:P * i + P], wp[:],
                                                    start=True, stop=True)
                        last.then_inc(bank_full[u[0]], 1)
                if g == 3 and live(n + -1):
                    b = n + -1
                    if t == 1:
                        pe.wait_ge(ln_step[0], b.times(4, 4))
                        transposes(use_of(b, "x1T"), [x1[:, i, :] for i in range(T)])
                    if 3 <= t < 7:
                        m = t - 3
                        if m == 0:
                            pe.wait_ge(split_ready, b.times(9, 1))
                            if b.reg is None and b.c == 0:
                                pe.wait_ge(setup_step, 9)
                        ffn(b, f"ffn0_{m}", [(w0[:, P * m:P * m + P], x1_hi[:], x1_lo[:])])

            def iteration(n):
                for g in range(G):
                    for t in range(STEPS):
                        if live(n):
                            scores(n, g, t)
                        if live(n + 1):
                            max_scores(n + 1, g, t)
                        if 1 <= t <= 4:
                            order = t - 1
                            kt = (0, 1, 3, 2)[order]
                            if g == 0 and live(n + -1):
                                sums(n + -1, 3, kt, order)
                            if g > 0 and live(n):
                                sums(n, g - 1, kt, order)
                        fill(n, g, t)

            run(pe, iteration)


_INS = ["L0_attn_hidden_states", "L0_attn_c_attn_w", "L0_attn_c_attn_b", "L0_attn_c_proj_w", "L0_attn_c_proj_b",
        "L0_ffn_k0", "L0_ffn_k1", "L0_ffn_k2", "L0_ffn_s0", "L0_ffn_s1", "L0_ffn_s2"]


def kernel(**inputs):
    import numpy as _np
    import concourse.bacc as _bacc
    from concourse import mybir as _mybir
    from concourse.bass_utils import run_bass_kernel_spmd as _run

    nc = _bacc.Bacc("TRN2", target_bir_lowering=False, num_devices=1)
    arrays, args = {}, []
    for name in _INS:
        a = _np.ascontiguousarray(inputs[name])
        arrays[f"in_{name}"] = a
        args.append(nc.dram_tensor(f"in_{name}", a.shape, _mybir.dt.from_np(a.dtype), kind="ExternalInput").ap())
    shape = arrays[f"in_{_INS[0]}"].shape
    args.append(nc.dram_tensor("out_x", shape, _mybir.dt.float32, kind="ExternalOutput").ap())
    block_kernel(nc, *args)
    r = _run(nc, [arrays], core_ids=[0])
    return r.results[0]["out_x"]
```

```python
from contextlib import ExitStack

import concourse.bass as bass
from concourse import mybir

F32 = mybir.dt.float32
F32R = mybir.dt.float32r
BF16 = mybir.dt.bfloat16
ALU = mybir.AluOpType
ACT = mybir.ActivationFunctionType
AX = mybir.AxisListType

HEADS = 16
FOCUS = 1.6
EPS = 1e-5
NEG = -3.0e38
TWO_ONES = 1.0 + 0x3F80 / 2.0 ** 23

BANK_USES = (
    ("ffn1_0", -2), ("negmax1", 0), ("ffn1_1", -2), ("ffn1_2", -2), ("v", 1), ("ffn1_3", -2), ("xT", 2),
    ("tok_0", -1), ("tok_1", -1), ("tok_2", -1), ("tok_3", -1), ("q", 2), ("k", 2), ("ffn2", -2),
    ("negmax0", 1), ("attnT", -1), ("proj", -1),
    ("x1T", -1), ("ffn0_0", -1), ("ffn0_1", -1), ("ffn0_2", -1), ("ffn0_3", -1),
)


UNROLL = 2


class At:

    def __init__(self, c, reg=None):
        self.c, self.reg = c, reg

    def __add__(self, k):
        return At(self.c + k, self.reg)

    def times(self, per, plus=0):
        k = self.c * per + plus
        return k if self.reg is None else self.reg * (UNROLL * per) + k

    @property
    def parity(self):
        return self.c % 2


def block_kernel(nc, x, w_qkv, b_qkv, w_proj, b_proj, k0, k1, k2, s0, s1, s2, out):
    B, S, D = x.shape
    H, R = HEADS, D // HEADS
    P = 128
    T = S // P
    F = k0.shape[1]
    FT = F // P
    SCALE = float(R) ** -0.5
    G = 4
    STEPS = 10
    HALF = H // 2
    MAX_RING = 3
    QK_ROWS, MAX_ROW = 96, 96
    ALL_ROWS = MAX_ROW + 3
    FIRST, LAST = -2, B + 1
    LOOP = (3, B - 3)
    assert (D, H, T, FT, R) == (128, 16, 4, 4, 8) and (LOOP[1] - LOOP[0]) % UNROLL == 0

    def live(b):
        return b.reg is not None or 0 <= b.c < B

    USES = len(BANK_USES)
    used_before = {FIRST: 0}
    for n in range(FIRST, LAST + 1):
        used_before[n + 1] = used_before[n] + sum(0 <= n + d < B for _, d in BANK_USES)
    assert used_before[LOOP[1]] - used_before[LOOP[0]] == USES * (LOOP[1] - LOOP[0]) and USES % 2 == 0

    def use(n, what):
        before = [d for w, d in BANK_USES[:[w for w, _ in BANK_USES].index(what)]]
        if n.reg is None:
            i = used_before[n.c] + sum(0 <= n.c + d < B for d in before)
            return i % 2, i // 2 + 1
        i = used_before[LOOP[0]] + USES * (n.c - LOOP[0]) + len(before)
        return i % 2, n.reg * (UNROLL * USES // 2) + (i // 2 + 1)

    def use_of(b, what):
        return use(b + -dict(BANK_USES)[what], what)

    with ExitStack() as ctx:
        def sb(name, shape, dt=F32):
            return ctx.enter_context(nc.sbuf_tensor(name, shape, dt))

        def sem(name):
            return ctx.enter_context(nc.semaphore(name))

        score_ps = ctx.enter_context(nc.psum_tensor("score_ps", [P, 2, S], F32))
        max_ps = ctx.enter_context(nc.psum_tensor("max_ps", [P, MAX_RING, S], F32))
        av_ps = ctx.enter_context(nc.psum_tensor("av_ps", [P, S], F32))
        bank_ps = ctx.enter_context(nc.psum_tensor("bank_ps", [P, 2, S], F32))

        ident = sb("ident", [P, P])
        ident_bf = sb("ident_bf", [P, P], BF16)
        future_bf = sb("future_bf", [P, P], BF16)
        mult = sb("mult", [P, T, 3])
        minus_half = sb("minus_half", [P, T])
        one = sb("one", [1, P])
        wc = sb("wc", [P, 3 * D])
        wqk = sb("wqk", [P, 2, P])
        wp = sb("wp", [P, D])
        bqk_row = sb("bqk_row", [1, 3 * D])
        bqk_perm = sb("bqk_perm", [1, 2, P])
        bqk = sb("bqk", [P, 2])
        bv = sb("bv", [P, D])
        bp = sb("bp", [P, D])
        scales = sb("scales", [P, 3])
        scales2 = sb("scales2", [P, 3])
        w0 = sb("w0", [P, F], F32R)
        w1 = sb("w1", [P, FT, F], F32R)
        w2 = sb("w2", [P, FT, D], F32R)

        stack = [sb(f"stack{i}", [P, H, 2, S], BF16) for i in range(2)]
        x_in = sb("x_in", [P, T, D])
        x_res = sb("x_res", [P, T, D])
        xT = sb("xT", [P, S])
        qk = sb("qk", [P, 2, S])
        parts = sb("parts", [P, 6, S], BF16)
        vaug = [sb(f"vaug{i}", [P, T, H, R + 1]) for i in range(2)]
        negmax = sb("negmax", [P, 2, T, HALF])
        negmax_rest = sb("negmax_rest", [P, 2, T, HALF])
        negmax_parts = sb("negmax_parts", [P, 2, T, 3, HALF], BF16)
        negmaxT = sb("negmaxT", [3 * HALF, 2, S], BF16)
        e = [sb(f"e{i}", [P, STEPS, S]) for i in range(2)]
        avT = sb("avT", [P, G, S])
        recip = sb("recip", [P, 2, H])
        attn = sb("attn", [P, T, D])
        attnT = sb("attnT", [P, S])
        res1 = sb("res1", [P, T, D])
        x1 = sb("x1", [P, T, D])
        stats = sb("stats", [P, 2, T, 6])
        moments = sb("moments", [P, 2, T, 2])
        var_eps = sb("var_eps", [P, 2, T])
        rstd = sb("rstd", [P, 2, T])
        full = sb("full", [P, 2, S])
        x1_hi = sb("x1_hi", [P, S], F32R)
        x1_lo = sb("x1_lo", [P, S], F32R)
        h_hi = [sb(f"h{i}_hi", [P, FT, S], F32R) for i in range(2)]
        h_lo = [sb(f"h{i}_lo", [P, FT, S], F32R) for i in range(2)]
        res2 = sb("res2", [P, T, D])

        raw0 = e[0][:, 0:2, :].rearrange("p a s -> p (a s)").bitcast(mybir.dt.uint8)[:, 0:2 * F]
        raw1 = e[0][:, 2:4, :].rearrange("p a s -> p (a s)").bitcast(mybir.dt.uint8)[:, 0:FT * F]
        raw2 = e[0][:, 4:5, :].rearrange("p a s -> p (a s)").bitcast(mybir.dt.uint8)[:, 0:FT * D]
        w0_half = e[0][:, 5, :]

        w_loaded = sem("w_loaded")
        ffn_loaded = sem("ffn_loaded")
        consts_step = sem("consts_step")
        consts_ready = sem("consts_ready")
        stack_cleared = [sem(f"stack{i}_cleared") for i in range(2)]
        setup_step = sem("setup_step")
        bias_row = sem("bias_row")
        x_loaded = sem("x_loaded")
        xres_loaded = sem("xres_loaded")
        xres_biased = sem("xres_biased")
        bank_full = [sem(f"bank{i}_full") for i in range(2)]
        bank_free = [sem(f"bank{i}_free") for i in range(2)]
        split_step = sem("split_step")
        stacked = [sem(f"stacked{i}") for i in range(2)]
        v_added = sem("v_added")
        v_ready = sem("v_ready")
        max_scored = sem("max_scored")
        max_taken = sem("max_taken")
        negmax_step = sem("negmax_step")
        negmax_in = [sem(f"negmax_in{i}") for i in range(2)]
        scored = sem("scored")
        exped = sem("exped")
        masked = sem("masked")
        summed = sem("summed")
        av_out = sem("av_out")
        recip_ready = sem("recip_ready")
        ln_step = [sem(f"ln{i + 1}_step") for i in range(2)]
        rstd_ready = [sem(f"rstd{i + 1}_ready") for i in range(2)]
        hi_ready = sem("hi_ready")
        split_ready = sem("split_ready")
        stored = sem("stored")

        x_tok = x.rearrange("b (t p) d -> b p t d", p=P)
        out_tok = out.rearrange("b (t p) d -> b p t d", p=P)

        block = ctx.enter_context(nc.Block())

        def run(eng, iteration):
            for n in range(FIRST, LOOP[0]):
                iteration(At(n))
            with eng.Fori(0, (LOOP[1] - LOOP[0]) // UNROLL) as i:
                for u in range(UNROLL):
                    iteration(At(LOOP[0] + u, i))
            for n in range(LOOP[1], LAST + 1):
                iteration(At(n))

        def wait_full(eng, u):
            eng.wait_ge(bank_full[u[0]], u[1])

        def wait_free(eng, u):
            eng.wait_ge(bank_free[u[0]], u[1])

        def apart(eng):
            eng.nop(nofuse=True)

        def full_slot(b, k):
            return (b.c * 9 + k) % 2

        @block.sync
        def _(sp):
            sp.dma_start(x_in[:], x_tok[0]).then_inc(x_loaded, 16)
            sp.dma_start(wc[:], w_qkv).then_inc(w_loaded, 16)
            sp.dma_start(bqk_row[:], b_qkv.rearrange("(a n) -> a n", a=1)).then_inc(w_loaded, 16)
            sp.dma_start(bv[:], b_qkv[2 * D:3 * D].partition_broadcast(P)).then_inc(w_loaded, 16)
            sp.dma_start(bp[:], b_proj.partition_broadcast(P)).then_inc(w_loaded, 16)
            sp.dma_start(wp[:], w_proj).then_inc(w_loaded, 16)
            sp.dma_start(raw0.rearrange("p (a n) -> p a n", a=2),
                         k0.rearrange("(a p) n -> p a n", p=P)).then_inc(ffn_loaded, 16)
            sp.dma_start(raw1.rearrange("p (a n) -> p a n", a=FT),
                         k1.rearrange("(a p) n -> p a n", p=P)).then_inc(ffn_loaded, 16)
            sp.dma_start(raw2.rearrange("p (a n) -> p a n", a=FT),
                         k2.rearrange("(a p) n -> p a n", p=P)).then_inc(ffn_loaded, 16)
            for i, s in enumerate((s0, s1, s2)):
                sp.dma_start(scales[:, i:i + 1], s.partition_broadcast(P)).then_inc(ffn_loaded, 16)

            def stack_half(b, half):
                for a in range(3):
                    for c in range(3):
                        row = R * (3 * a + c)
                        src = parts[64 * half:64 * half + 64, c:3 + a + 1:3 + a - c, :]
                        sp.dma_start(stack[b.parity][row:row + R, HALF * half:HALF * half + HALF, :, :],
                                     src).then_inc(stacked[half], 16)

            def negmax_rows(b, half):
                wait_free(sp, use_of(b, f"negmax{half}"))
                sp.dma_start(stack[b.parity][MAX_ROW:ALL_ROWS, HALF * half:HALF * half + HALF, 0, :],
                             negmaxT[:, half, :]).then_inc(negmax_in[half], 16)

            def iteration(n):
                b = n + 2
                if live(b) and not (b.reg is None and b.c == 0):
                    wait_full(sp, use_of(b + -1, "xT"))
                    sp.dma_start(x_in[:], x_tok[b.times(1)]).then_inc(x_loaded, 16)
                b = n + -1
                if live(b):
                    if b.c > 0 or b.reg is not None:
                        wait_free(sp, use_of(b + -1, "proj"))
                    sp.dma_start(x_res[:], x_tok[b.times(1)]).then_inc(xres_loaded, 16)
                if live(n):
                    negmax_rows(n, 1)
                b = n + -2
                if live(b):
                    sp.wait_ge(ln_step[1], b.times(4, 4))
                    sp.dma_start(out_tok[b.times(1)], res2[:]).then_inc(stored, 16)
                if live(n + 1):
                    negmax_rows(n + 1, 0)
                b = n + 2
                if live(b):
                    sp.wait_ge(split_step, b.times(3, 3))
                    apart(sp)
                    if live(n):
                        sp.wait_ge(scored, n.times(G * STEPS, 2 * STEPS))
                    else:
                        sp.wait_ge(stack_cleared[b.parity], 2)
                    stack_half(b, 0)
                    if live(n):
                        sp.wait_ge(scored, n.times(G * STEPS, 4 * STEPS))
                    stack_half(b, 1)

            run(sp, iteration)
            sp.wait_ge(stored, 16 * B)

        @block.gpsimd
        def _(pool):
            step = 0
            for t, v in ((ident, 0.0), (ident_bf, 0.0), (future_bf, 0.0), (mult, FOCUS)):
                nc.gpsimd.memset(t[:], v).then_inc(consts_step, 1)
                step += 1
            nc.gpsimd.memset(minus_half[:], -0.5).then_inc(consts_step, 1)
            nc.gpsimd.memset(one[:], 1.0).then_inc(consts_step, 1)
            step += 2
            pool.wait_ge(consts_step, step)
            for t in (ident, ident_bf):
                nc.gpsimd.affine_select(out=t[:], in_=t[:], compare_op=ALU.not_equal, fill=1.0, base=0,
                                        pattern=[[-1, P]], channel_multiplier=1).then_inc(consts_step, 1)
            nc.gpsimd.affine_select(out=future_bf[:], in_=future_bf[:], compare_op=ALU.is_ge, fill=NEG, base=0,
                                    pattern=[[1, P]], channel_multiplier=-1).then_inc(consts_step, 1)
            first_end = max(1, S // 3)
            second_end = max(first_end + 1, 2 * S // 3)
            step += 3
            for h, base, sign in ((0, first_end - 1, -1), (1, -first_end, 1), (2, -second_end, 1),
                                  (1, second_end - 1, -1)):
                pool.wait_ge(consts_step, step)
                nc.gpsimd.affine_select(out=mult[:, :, h:h + 1], in_=mult[:, :, h:h + 1], compare_op=ALU.is_ge,
                                        fill=1.0, base=base, pattern=[[sign * P, T], [0, 1]],
                                        channel_multiplier=sign).then_inc(consts_step, 1)
                step += 1
            pool.wait_ge(consts_step, step)
            nc.gpsimd.memset(recip[:], 1.0).then_inc(consts_ready, 1)
            pool.wait_ge(consts_ready, 1)
            nc.gpsimd.memset(stack[1][64:P].rearrange("p h a s -> p (h a s)").bitcast(F32),
                             0.0).then_inc(stack_cleared[1], 1)
            pool.wait_ge(stack_cleared[1], 1)
            nc.gpsimd.memset(stack[1][MAX_ROW:P, :, 1, :].bitcast(F32), TWO_ONES).then_inc(stack_cleared[1], 1)
            pool.wait_ge(stack_cleared[1], 2)

            def split(b, k):
                if k == 0:
                    wait_free(pool, use_of(b, "q"))
                    wait_free(pool, use_of(b, "k"))
                else:
                    pool.wait_ge(split_step, b.times(3, k))
                if k == 0:
                    ins = nc.gpsimd.tensor_tensor(qk[:], qk[:], parts[:, 0:4:3, :], ALU.subtract)
                else:
                    ins = nc.gpsimd.tensor_tensor(parts[:, 2:6:3, :], qk[:], parts[:, 1:5:3, :], ALU.subtract)
                ins.then_inc(split_step, 1)

            def mask(n, g, k):
                buf = e[g % 2]
                if k == 0:
                    after, blocks = 4, (buf[:, 0:4, 0:P],)
                elif k == 1:
                    after, blocks = 8, (buf[:, 4:8, 0:P], buf[:, 4:8, 3 * P:S])
                else:
                    halves = buf[:, 8:10, :].rearrange("p h (a c) -> p (h a) c", c=2 * P)
                    after, blocks = 10, (halves[:, :, 0:P],)
                pool.wait_ge(exped, n.times(G * STEPS, STEPS * g + after))
                apart(pool)
                for ap in blocks:
                    last = nc.gpsimd.affine_select(out=ap, in_=ap, compare_op=ALU.is_ge, fill=0.0, base=0,
                                                   pattern=[[0, 4], [1, P]], channel_multiplier=-1)
                last.then_inc(masked, 1)

            def low_part(b, layer, m):
                k = 1 + FT * layer + m
                pool.wait_ge(hi_ready, b.times(9, k + 1))
                nc.gpsimd.tensor_tensor(h_lo[layer][:, m, :], full[:, full_slot(b, k), :],
                                        h_hi[layer][:, m, :].bitcast(F32), ALU.subtract).then_inc(split_ready, 1)

            def rstd_of(b, i):
                pool.wait_ge(ln_step[i], b.times(4, 3))
                nc.gpsimd.tensor_tensor(rstd[:, i, :], var_eps[:, i, :], minus_half[:],
                                        ALU.pow).then_inc(rstd_ready[i], 1)

            def iteration(n):
                def low(layer, *ms):
                    b = n + (-2 if layer else -1)
                    for m in ms:
                        if live(b):
                            low_part(b, layer, m)

                def masks(g, k):
                    if live(n):
                        mask(n, g, k)

                masks(0, 0)
                low(1, 0, 1)
                masks(0, 1)
                low(1, 2)
                masks(0, 2)
                low(1, 3)

                masks(1, 0)
                if live(n + -1):
                    b = n + -1
                    pool.wait_ge(xres_loaded, b.times(16, 16))
                    nc.gpsimd.tensor_tensor(x_res[:], x_res[:], bp[:].unsqueeze(1).broadcast_to([P, T, D]),
                                            ALU.add).then_inc(xres_biased, 1)
                masks(1, 1)
                if live(n + 2):
                    split(n + 2, 0)
                masks(1, 2)

                if live(n + -2):
                    rstd_of(n + -2, 1)
                masks(2, 0)
                if live(n + 2):
                    split(n + 2, 2)
                masks(2, 1)
                if live(n + -1):
                    rstd_of(n + -1, 0)
                masks(2, 2)

                masks(3, 0)
                low(0, 0, 1)
                masks(3, 1)
                low(0, 2, 3)
                masks(3, 2)

            pool.wait_ge(w_loaded, 16 * 5)
            run(pool, iteration)

        @block.scalar
        def _(act):
            act.wait_ge(setup_step, 9)

            def take(u, out_ap, func, **kw):
                wait_full(act, u)
                nc.scalar.activation(out_ap, bank_ps[:, u[0], :], func, **kw).then_inc(bank_free[u[0]], 1)

            def exp(n, g, t):
                act.wait_ge(scored, n.times(G * STEPS, STEPS * g + t + 1))
                if t == 0 and not (n.reg is None and n.c * G + g < 2):
                    act.wait_ge(summed, n.times(G, g - 1))
                nc.scalar.activation(e[g % 2][:, t, :], score_ps[:, t % 2, :], ACT.Exp,
                                     scale=SCALE).then_inc(exped, 1)

            def sums_out(b, g):
                act.wait_ge(summed, b.times(G, g + 1))
                if g == 0 and (b.reg is not None or b.c > 0):
                    wait_full(act, use_of(b + -1, "tok_3"))
                nc.scalar.activation(avT[:, g, :], av_ps[:], ACT.Copy).then_inc(av_out, 1)

            def activation_out(b, k, what, func, **kw):
                if b.reg is not None or b.c * 9 + k >= 2:
                    act.wait_ge(split_ready, b.times(9, k - 1))
                take(use_of(b, what), full[:, full_slot(b, k), :], func, **kw)

            def iteration(n):
                for g in range(G):
                    for t in range(STEPS):
                        if live(n):
                            exp(n, g, t)
                        if t == 5:
                            if g == 0 and live(n + -1):
                                sums_out(n + -1, 3)
                            if g > 0 and live(n):
                                sums_out(n, g - 1)
                        if g == 0 and t in (2, 4, 6, 8) and live(n + -2):
                            m = t // 2 - 1
                            activation_out(n + -2, 5 + m, f"ffn1_{m}", ACT.Relu, scale=scales2[:, 1:2])
                        if g == 0 and t == 9 and live(n + 2):
                            if live(n + 1):
                                wait_full(act, use_of(n + 1, "v"))
                            take(use_of(n + 2, "xT"), xT[:], ACT.Copy)
                        if g == 1 and t in (5, 6) and live(n + 2):
                            b, i = n + 2, t - 5
                            if i == 0 and (b.reg is not None or b.c > 0):
                                for half in range(2):
                                    act.wait_ge(stacked[half], b.times(9 * 16))
                            u = use_of(b, "qk"[i])
                            wait_full(act, u)
                            nc.scalar.activation(parts[:, 3 * i, :], bank_ps[:, u[0], :], ACT.Identity,
                                                 bias=bqk[:, i:i + 1])
                            take(u, qk[:, i, :], ACT.Identity, bias=bqk[:, i:i + 1])
                        if g == 2 and t == 2 and live(n + 2):
                            act.wait_ge(split_step, (n + 2).times(3, 1))
                            nc.scalar.activation(parts[:, 1:5:3, :], qk[:], ACT.Copy).then_inc(split_step, 1)
                        if g == 2 and t == 3 and live(n + -1):
                            take(use_of(n + -1, "attnT"), attnT[:], ACT.Copy)
                        if g == 3 and t == 1 and live(n + -1):
                            activation_out(n + -1, 0, "x1T", ACT.Copy)
                        if g == 3 and 4 <= t < 8 and live(n + -1):
                            activation_out(n + -1, 1 + t - 4, f"ffn0_{t - 4}", ACT.Relu, scale=scales[:, 0:1])

            run(act, iteration)

        @block.vector
        def _(dve):
            nc.vector.memset(av_ps[:], 0.0).then_inc(setup_step, 1)
            for i in range(2):
                nc.vector.memset(vaug[i][:, :, :, R:R + 1], 1.0).then_inc(setup_step, 1)
            dve.wait_ge(w_loaded, 16 * 5)
            for i in range(2):
                for half in range(2):
                    cols = slice(D * i + 64 * half, D * i + 64 * half + 64)
                    ws = wc[:, cols].rearrange("p (h r) -> p r h", r=R)
                    bs = bqk_row[:, cols].rearrange("p (h r) -> p r h", r=R)
                    nc.vector.tensor_copy(
                        wqk[:, i, 64 * half:64 * half + 64].rearrange("p (r h) -> p r h", r=R), ws)
                    last = nc.vector.tensor_copy(
                        bqk_perm[:, i, 64 * half:64 * half + 64].rearrange("p (r h) -> p r h", r=R), bs)
            last.then_inc(setup_step, 1)
            dve.wait_ge(consts_ready, 1)
            dve.wait_ge(setup_step, 4)
            for i in range(2):
                last = nc.vector.tensor_copy(vaug[i][:, :, 0:3, R:R + 1], mult[:].unsqueeze(3))
            last.then_inc(setup_step, 1)
            dve.wait_ge(bias_row, 1)
            nc.vector.tensor_copy(bqk[:], max_ps[:, 0, 0:2]).then_inc(setup_step, 1)
            nc.vector.memset(stack[0][64:P].rearrange("p h a s -> p (h a s)").bitcast(F32),
                             0.0).then_inc(stack_cleared[0], 1)
            dve.wait_ge(stack_cleared[0], 1)
            nc.vector.memset(stack[0][MAX_ROW:P, :, 1, :].bitcast(F32), TWO_ONES).then_inc(stack_cleared[0], 1)
            dve.wait_ge(ffn_loaded, 16 * 6)
            nc.vector.tensor_scalar(scales2[:], scales[:], 2.0, None, ALU.mult).then_inc(setup_step, 1)
            nc.vector.tensor_scalar(w0_half, raw0[:, F:2 * F], -2.0, None, ALU.mult).then_inc(setup_step, 1)
            dve.wait_ge(setup_step, 8)
            nc.vector.scalar_tensor_tensor(w0[:], raw0[:, 0:F], 2.0, w0_half, ALU.mult, ALU.add)
            nc.vector.tensor_scalar(w1[:].rearrange("p a n -> p (a n)"), raw1, 2.0, -1.0, ALU.mult, ALU.add)
            nc.vector.tensor_scalar(w2[:].rearrange("p a n -> p (a n)"), raw2, 2.0, -1.0, ALU.mult,
                                    ALU.add).then_inc(setup_step, 1)

            def take_max(b, g, t):
                buf = max_ps[:, (STEPS * g + t) % MAX_RING, :]
                half, h = g // 2, G * (g % 2)
                dve.wait_ge(max_scored, b.times(G * STEPS, STEPS * g + t + 1))
                if t < 4:
                    ins = nc.vector.reduce_max(negmax[:, half, 3, h + t:h + t + 1], buf, AX.X, negate=True)
                elif t < 8:
                    i = h + t - 4
                    nc.vector.reduce_max(negmax[:, half, 2, i:i + 1], buf[:, 0:3 * P], AX.X, negate=True)
                    ins = nc.vector.reduce_max(negmax[:, half, 0, i:i + 1], buf[:, 3 * P:S], AX.X, negate=True)
                else:
                    i = h + 2 * (t - 8)
                    ins = nc.vector.reduce_max(negmax[:, half, 1, i:i + 2],
                                               buf.rearrange("p (h k) -> p h k", h=2), AX.X, negate=True)
                ins.then_inc(max_taken, 1)

            def split_negmax(b, half):
                m, r = negmax[:, half], negmax_rest[:, half]
                hi, mid, lo = (negmax_parts[:, half, :, i, :] for i in range(3))
                dve.wait_ge(max_taken, b.times(G * STEPS, 2 * STEPS * (half + 1)))
                for k in range(4):
                    if k:
                        dve.wait_ge(negmax_step, b.times(8, 4 * half + k))
                    if k == 0:
                        ins = nc.vector.tensor_copy(hi, m)
                    elif k == 1:
                        ins = nc.vector.tensor_tensor(r, m, hi, ALU.subtract)
                    elif k == 2:
                        ins = nc.vector.tensor_copy(mid, r)
                    else:
                        ins = nc.vector.tensor_tensor(lo, r, mid, ALU.subtract)
                    ins.then_inc(negmax_step, 1)

            def take_negmaxT(b, half):
                u = use_of(b, f"negmax{half}")
                wait_full(dve, u)
                if b.reg is not None or b.c > 0:
                    dve.wait_ge(negmax_in[half], b.times(16))
                src = bank_ps[0:3 * HALF, u[0], :].bitcast(BF16)[:, 0:S]
                nc.vector.tensor_copy(negmaxT[:, half, :], src).then_inc(bank_free[u[0]], 1)

            def take_v(b):
                u = use_of(b, "v")
                wait_full(dve, u)
                va = vaug[b.parity]
                if b.reg is not None or b.c > 1:
                    dve.wait_ge(summed, b.times(G, -G))
                nc.vector.tensor_tensor(va[:, :, :, 0:R], bank_ps[:, u[0], :].rearrange("p (t h r) -> p t h r", t=T, r=R),
                                        bv[:].rearrange("p (h r) -> p h r", r=R).unsqueeze(1).broadcast_to([P, T, H, R]),
                                        ALU.add).then_inc(bank_free[u[0]], 1)
                wait_free(dve, u)
                nc.vector.tensor_tensor(va[:, :, 0:3, 0:R], va[:, :, 0:3, 0:R],
                                        mult[:].unsqueeze(3).broadcast_to([P, T, 3, R]), ALU.mult).then_inc(v_ready, 1)

            def normalise(b, t):
                u = use_of(b, f"tok_{t}")
                wait_full(dve, u)
                src = bank_ps[:, u[0], :].rearrange("p (h c) -> p h c", c=32)
                nc.vector.reciprocal(recip[:, t % 2, :].unsqueeze(2), src[:, :, R:R + 1]).then_inc(recip_ready, 1)
                dve.wait_ge(recip_ready, b.times(T, t + 1))
                nc.vector.tensor_tensor(attn[:, t, :].rearrange("p (h r) -> p h r", r=R), src[:, :, 0:R],
                                        recip[:, t % 2, :].unsqueeze(2).broadcast_to([P, H, R]),
                                        ALU.mult).then_inc(bank_free[u[0]], 1)

            def layernorm_stats(i, src, u):
                wait_free(dve, u)
                for t in range(T):
                    ins = nc.vector.bn_stats(stats[:, i, t, :], src[:, t, :])
                ins.then_inc(ln_step[i], 1)

            def layernorm_var(b, i):
                dve.wait_ge(ln_step[i], b.times(4, 1))
                apart(dve)
                for t in range(T):
                    ins = nc.vector.bn_aggr(moments[:, i, t, :], stats[:, i, t, :])
                ins.then_inc(ln_step[i], 1)
                dve.wait_ge(ln_step[i], b.times(4, 2))
                nc.vector.tensor_scalar(var_eps[:, i, :].unsqueeze(2), moments[:, i, :, 1:2], EPS, None,
                                        ALU.add).then_inc(ln_step[i], 1)

            def layernorm_out(b, i, src, dst):
                dve.wait_ge(rstd_ready[i], b.times(1, 1))
                for t in range(T):
                    ins = nc.vector.tensor_scalar(dst[:, t, :], src[:, t, :], moments[:, i, t, 0:1],
                                                  rstd[:, i, t:t + 1], ALU.subtract, ALU.mult)
                ins.then_inc(ln_step[i], 1)

            def high_part(b, k, hi, what):
                wait_free(dve, use_of(b, what))
                nc.vector.tensor_copy(hi, full[:, full_slot(b, k), :]).then_inc(hi_ready, 1)

            def low_part(b, k, hi, lo):
                dve.wait_ge(hi_ready, b.times(9, k + 1))
                nc.vector.tensor_tensor(lo, full[:, full_slot(b, k), :], hi.bitcast(F32),
                                        ALU.subtract).then_inc(split_ready, 1)

            def iteration(n):
                for g in range(G):
                    for t in range(STEPS):
                        if live(n + 1):
                            take_max(n + 1, g, t)
                        if g == 0:
                            if t in (3, 5, 7, 9) and live(n + -2):
                                m = (t - 3) // 2
                                high_part(n + -2, 5 + m, h_hi[1][:, m, :], f"ffn1_{m}")
                            if t == 4 and live(n):
                                take_negmaxT(n, 1)
                            if t == 8 and live(n + 1):
                                take_v(n + 1)
                        if g == 1:
                            if 1 <= t <= 4 and live(n + -1):
                                normalise(n + -1, t - 1)
                            if t == 7 and live(n + -2):
                                b = n + -2
                                u = use_of(b, "ffn2")
                                wait_full(dve, u)
                                if b.reg is not None or b.c > 0:
                                    dve.wait_ge(stored, b.times(16))
                                nc.vector.scalar_tensor_tensor(
                                    res2[:].rearrange("p t d -> p (t d)"), bank_ps[:, u[0], :], scales2[:, 2:3],
                                    x1[:].rearrange("p t d -> p (t d)"), ALU.mult, ALU.add).then_inc(bank_free[u[0]], 1)
                                layernorm_stats(1, res2, u)
                            if t == 9 and live(n + 1):
                                split_negmax(n + 1, 0)
                            if t == 8 and live(n + -2):
                                layernorm_var(n + -2, 1)
                        if g == 2:
                            if t == 1 and live(n + -2):
                                layernorm_out(n + -2, 1, res2, res2)
                            if t == 3 and live(n + 1):
                                take_negmaxT(n + 1, 0)
                            if t == 5 and live(n + -1):
                                b = n + -1
                                u = use_of(b, "proj")
                                wait_full(dve, u)
                                dve.wait_ge(xres_biased, b.times(1, 1))
                                nc.vector.tensor_tensor(res1[:].rearrange("p t d -> p (t d)"), bank_ps[:, u[0], :],
                                                        x_res[:].rearrange("p t d -> p (t d)"),
                                                        ALU.add).then_inc(bank_free[u[0]], 1)
                                layernorm_stats(0, res1, u)
                            if t == 6 and live(n + -1):
                                layernorm_var(n + -1, 0)
                            if t == 9 and live(n + -1):
                                layernorm_out(n + -1, 0, res1, x1)
                        if g == 3:
                            if t == 2 and live(n + -1):
                                high_part(n + -1, 0, x1_hi[:], "x1T")
                                low_part(n + -1, 0, x1_hi[:], x1_lo[:])
                            if 5 <= t < 9 and live(n + -1):
                                m = t - 5
                                high_part(n + -1, 1 + m, h_hi[0][:, m, :], f"ffn0_{m}")
                            if t == 9 and live(n + 1):
                                split_negmax(n + 1, 1)

            run(dve, iteration)

        @block.tensor
        def _(pe):
            pe.wait_ge(setup_step, 4)
            pe.wait_ge(consts_ready, 1)
            for i in range(2):
                last = nc.tensor.matmul(max_ps[:, 0, i:i + 1], bqk_perm[0:1, i, :], one[0:1, 0:1],
                                        start=(i == 0), stop=True, skip_group_check=True)
            last.then_inc(bias_row, 1)
            pe.wait_ge(setup_step, 6)

            def claim(u):
                if not (isinstance(u[1], int) and u[1] == 1):
                    pe.wait_ge(bank_free[u[0]], u[1] + -1)
                return bank_ps[:, u[0], :]

            def transposes(u, sources, into=None):
                bank = claim(u)
                for i, src in enumerate(sources):
                    last = nc.tensor.transpose(bank[:, P * i:P * i + P], src, ident[:])
                last.then_inc(bank_full[u[0]], 1)

            def max_scores(b, g, t):
                i = STEPS * g + t
                st, out_ap = stack[b.parity], max_ps[:, i % MAX_RING, :]
                if t == 0 and g % 2 == 0:
                    pe.wait_ge(stacked[g // 2], b.times(9 * 16, 9 * 16))
                last_use = i - MAX_RING
                if i < MAX_RING:
                    last_use = max(j - G * STEPS for j in range(G * STEPS) if j % MAX_RING == i)
                if not (b.reg is None and b.c == 0 and last_use < 0):
                    pe.wait_ge(max_taken, b.times(G * STEPS, last_use + 1))

                def part(h, qt, col):
                    width = P * (qt + 1)
                    nc.tensor.matmul(out_ap[:, col:col + width], st[0:QK_ROWS, h, 0, P * qt:P * qt + P],
                                     st[0:QK_ROWS, h, 1, 0:width], start=True, stop=False)
                    return nc.tensor.matmul(out_ap[:, col + width - P:col + width], future_bf[:], ident_bf[:],
                                            start=False, stop=True)
                if t < 4:
                    last = part(G * g + t, 3, 0)
                elif t < 8:
                    part(G * g + t - 4, 2, 0)
                    last = part(G * g + t - 4, 0, 3 * P)
                else:
                    part(G * g + 2 * (t - 8), 1, 0)
                    last = part(G * g + 2 * (t - 8) + 1, 1, 2 * P)
                last.then_inc(max_scored, 1)

            def scores(n, g, t):
                st, out_ap = stack[n.parity], score_ps[:, t % 2, :]
                if t == 0 and g % 2 == 0:
                    pe.wait_ge(negmax_in[g // 2], n.times(16, 16))
                if not (n.reg is None and n.c == 0 and g == 0 and t < 2):
                    pe.wait_ge(exped, n.times(G * STEPS, STEPS * g + t - 1))

                def part(h, kt, col):
                    width = S - P * kt
                    return nc.tensor.matmul(out_ap[:, col:col + width], st[0:ALL_ROWS, h, 1, P * kt:P * kt + P],
                                            st[0:ALL_ROWS, h, 0, P * kt:S], start=True, stop=True)
                if t < 4:
                    last = part(G * g + t, 0, 0)
                elif t < 8:
                    part(G * g + t - 4, 1, 0)
                    last = part(G * g + t - 4, 3, 3 * P)
                else:
                    part(G * g + 2 * (t - 8), 2, 0)
                    last = part(G * g + 2 * (t - 8) + 1, 2, 2 * P)
                last.then_inc(scored, 1)

            def sums(b, g, kt, order):
                if order == 0:
                    pe.wait_ge(masked, b.times(3 * G, 3 * g + 1))
                    if g == 0:
                        pe.wait_ge(v_ready, b.times(1, 1))
                    if not (b.reg is None and b.c == 0 and g == 0):
                        pe.wait_ge(av_out, b.times(G, g))
                elif order == 1:
                    pe.wait_ge(masked, b.times(3 * G, 3 * g + 2))
                elif order == 3:
                    pe.wait_ge(masked, b.times(3 * G, 3 * g + 3))
                for j in range(G):
                    if kt == 0:
                        src = e[g % 2][:, j, :]
                    elif kt == 1:
                        src = e[g % 2][:, 4 + j, 0:3 * P]
                    elif kt == 3:
                        src = e[g % 2][:, 4 + j, 3 * P:S]
                    else:
                        src = e[g % 2][:, 8 + j // 2, 2 * P * (j % 2):2 * P * (j % 2) + 2 * P]
                    last = nc.tensor.matmul(av_ps[32 * j:32 * j + R + 1, P * kt:S],
                                            vaug[b.parity][:, kt, G * g + j, :], src,
                                            start=(order == 0), stop=(order == 3))
                if order == 3:
                    last.then_inc(summed, 1)

            def negmax_transposes(b, half):
                u = use_of(b, f"negmax{half}")
                pe.wait_ge(negmax_step, b.times(8, 4 * half + 4))
                bank = claim(u).bitcast(BF16)
                for qt in range(T):
                    last = nc.tensor.transpose(bank[0:3 * HALF, P * qt:P * qt + P],
                                               negmax_parts[:, half, qt].rearrange("p c h -> p (c h)"), ident_bf[:])
                last.then_inc(bank_full[u[0]], 1)

            def token_transposes(b, t):
                if t == 0:
                    pe.wait_ge(av_out, b.times(G, G))
                transposes(use_of(b, f"tok_{t}"), [avT[:, g, P * t:P * t + P] for g in range(G)])

            def ffn(b, what, pairs):
                u = use_of(b, what)
                bank = claim(u)
                for i, (w, hi, lo) in enumerate(pairs):
                    nc.tensor.matmul(bank, w, hi, start=(i == 0), stop=False)
                    last = nc.tensor.matmul(bank, w, lo, start=False, stop=(i == len(pairs) - 1))
                last.then_inc(bank_full[u[0]], 1)

            def fill(n, g, t):
                if g == 0:
                    if t == 3 and live(n):
                        negmax_transposes(n, 1)
                    if t in (2, 4, 6, 8) and live(n + -2):
                        m, b = t // 2 - 1, n + -2
                        if m == 0:
                            pe.wait_ge(split_ready, b.times(9, 5))
                        ffn(b, f"ffn1_{m}", [(w1[:, k, P * m:P * m + P], h_hi[0][:, k, :], h_lo[0][:, k, :])
                                             for k in range(FT)])
                    if t == 7 and live(n + 1):
                        u = use_of(n + 1, "v")
                        bank = claim(u)
                        wait_free(pe, use_of(n + 1, "xT"))
                        for kt in range(T):
                            last = nc.tensor.matmul(bank[:, P * kt:P * kt + P], xT[:, P * kt:P * kt + P],
                                                    wc[:, 2 * D:3 * D], start=True, stop=True)
                        last.then_inc(bank_full[u[0]], 1)
                    if t == 9 and live(n + 2):
                        pe.wait_ge(x_loaded, (n + 2).times(16, 16))
                        transposes(use_of(n + 2, "xT"), [x_in[:, i, :] for i in range(T)])
                if g == 1:
                    if 1 <= t <= 4 and live(n + -1):
                        token_transposes(n + -1, t - 1)
                    if t in (5, 6) and live(n + 2):
                        b, i = n + 2, t - 5
                        u = use_of(b, "qk"[i])
                        bank = claim(u)
                        wait_free(pe, use_of(b, "xT"))
                        nc.tensor.matmul(bank, wqk[:, i, :], xT[:], start=True, stop=True).then_inc(bank_full[u[0]], 1)
                    if t == 7 and live(n + -2):
                        b = n + -2
                        u = use_of(b, "ffn2")
                        pe.wait_ge(split_ready, b.times(9, 9))
                        bank = claim(u)
                        for qt in range(T):
                            col = slice(P * qt, P * qt + P)
                            for k in range(FT):
                                nc.tensor.matmul(bank[:, col], h_hi[1][:, k, col], w2[:, k, :],
                                                 start=(k == 0), stop=False)
                                last = nc.tensor.matmul(bank[:, col], h_lo[1][:, k, col], w2[:, k, :],
                                                        start=False, stop=(k == FT - 1))
                        last.then_inc(bank_full[u[0]], 1)
                if g == 2:
                    if t == 2 and live(n + 1):
                        negmax_transposes(n + 1, 0)
                    if t == 3 and live(n + -1):
                        wait_free(pe, use_of(n + -1, "tok_3"))
                        transposes(use_of(n + -1, "attnT"), [attn[:, i, :] for i in range(T)])
                    if t == 5 and live(n + -1):
                        u = use_of(n + -1, "proj")
                        bank = claim(u)
                        wait_free(pe, use_of(n + -1, "attnT"))
                        for i in range(T):
                            last = nc.tensor.matmul(bank[:, P * i:P * i + P], attnT[:, P * i:P * i + P], wp[:],
                                                    start=True, stop=True)
                        last.then_inc(bank_full[u[0]], 1)
                if g == 3 and live(n + -1):
                    b = n + -1
                    if t == 1:
                        pe.wait_ge(ln_step[0], b.times(4, 4))
                        transposes(use_of(b, "x1T"), [x1[:, i, :] for i in range(T)])
                    if 4 <= t < 8:
                        m = t - 4
                        if m == 0:
                            pe.wait_ge(split_ready, b.times(9, 1))
                            if b.reg is None and b.c == 0:
                                pe.wait_ge(setup_step, 9)
                        ffn(b, f"ffn0_{m}", [(w0[:, P * m:P * m + P], x1_hi[:], x1_lo[:])])

            def iteration(n):
                for g in range(G):
                    for t in range(STEPS):
                        if live(n):
                            scores(n, g, t)
                        if live(n + 1):
                            max_scores(n + 1, g, t)
                        if 1 <= t <= 4:
                            order = t - 1
                            kt = (0, 1, 3, 2)[order]
                            if g == 0 and live(n + -1):
                                sums(n + -1, 3, kt, order)
                            if g > 0 and live(n):
                                sums(n, g - 1, kt, order)
                        fill(n, g, t)

            run(pe, iteration)


_INS = ["L0_attn_hidden_states", "L0_attn_c_attn_w", "L0_attn_c_attn_b", "L0_attn_c_proj_w", "L0_attn_c_proj_b",
        "L0_ffn_k0", "L0_ffn_k1", "L0_ffn_k2", "L0_ffn_s0", "L0_ffn_s1", "L0_ffn_s2"]


def kernel(**inputs):
    import numpy as _np
    import concourse.bacc as _bacc
    from concourse import mybir as _mybir
    from concourse.bass_utils import run_bass_kernel_spmd as _run

    nc = _bacc.Bacc("TRN2", target_bir_lowering=False, num_devices=1)
    arrays, args = {}, []
    for name in _INS:
        a = _np.ascontiguousarray(inputs[name])
        arrays[f"in_{name}"] = a
        args.append(nc.dram_tensor(f"in_{name}", a.shape, _mybir.dt.from_np(a.dtype), kind="ExternalInput").ap())
    shape = arrays[f"in_{_INS[0]}"].shape
    args.append(nc.dram_tensor("out_x", shape, _mybir.dt.float32, kind="ExternalOutput").ap())
    block_kernel(nc, *args)
    r = _run(nc, [arrays], core_ids=[0])
    return r.results[0]["out_x"]
```

```python
from contextlib import ExitStack

import concourse.bass as bass
from concourse import mybir

F32 = mybir.dt.float32
F32R = mybir.dt.float32r
BF16 = mybir.dt.bfloat16
ALU = mybir.AluOpType
ACT = mybir.ActivationFunctionType
AX = mybir.AxisListType

HEADS = 16
FOCUS = 1.6
EPS = 1e-5
NEG = -3.0e38
TWO_ONES = 1.0 + 0x3F80 / 2.0 ** 23

PLACES = (
    ("negmax1", 0, (0, 3), (0, 4)),
    ("ffn1_0", -2, (0, 4), (0, 4)),
    ("ffn1_1", -2, (0, 4), (0, 4)),
    ("ffn1_2", -2, (0, 6), (0, 6)),
    ("v", 1, (0, 7), (0, 8)),
    ("ffn1_3", -2, (0, 9), (0, 9)),
    ("xT", 2, (0, 9), (0, 9)),
    ("tok_0", -1, (1, 1), (1, 1)),
    ("tok_1", -1, (1, 2), (1, 2)),
    ("tok_2", -1, (1, 2), (1, 3)),
    ("tok_3", -1, (1, 5), (1, 5)),
    ("q", 2, (1, 5), (1, 5)),
    ("k", 2, (1, 6), (1, 6)),
    ("ffn2T", -2, (1, 8), (2, 0)),
    ("ffn2", -2, (2, 2), (2, 3)),
    ("attnT", -1, (2, 3), (2, 3)),
    ("negmax0", 1, (2, 3), (2, 4)),
    ("proj", -1, (2, 6), (2, 6)),
    ("x1T", -1, (3, 2), (3, 2)),
    ("ffn0_0", -1, (3, 5), (3, 5)),
    ("ffn0_1", -1, (3, 5), (3, 5)),
    ("ffn0_2", -1, (3, 8), (3, 8)),
    ("ffn0_3", -1, (3, 9), (3, 9)),
)
BANK_USES = tuple((what, batch) for what, batch, _, _ in PLACES)
FFN2_STEPS = ((1, 8), (1, 8), (1, 9), (1, 9))
HIGH_STEPS = {"ffn1_0": (0, 4), "ffn1_1": (0, 5), "ffn1_2": (0, 7), "ffn1_3": (1, 3),
              "x1T": (3, 3), "ffn0_0": (3, 5), "ffn0_1": (3, 6), "ffn0_2": (3, 9), "ffn0_3": (3, 9)}
MIDDLE_STEP = (2, 2)
NEGMAX_SPLIT = (((2, 0), (2, 0), (2, 1), (2, 2)), ((0, 0), (0, 0), (0, 1), (0, 2)))
LN_VAR = ((2, 7), (2, 3))
LN_OUT = (((3, 0), (3, 0), (3, 0), (3, 0)), ((2, 7), (2, 7), (2, 7), (2, 7)))
SUM_STEPS = (1, 3, 5, 7)
SUMS_OUT = 9
UNROLL = 2


class At:

    def __init__(self, c, reg=None):
        self.c, self.reg = c, reg

    def __add__(self, k):
        return At(self.c + k, self.reg)

    def times(self, per, plus=0):
        k = self.c * per + plus
        return k if self.reg is None else self.reg * (UNROLL * per) + k

    @property
    def parity(self):
        return self.c % 2


def block_kernel(nc, x, w_qkv, b_qkv, w_proj, b_proj, k0, k1, k2, s0, s1, s2, out):
    B, S, D = x.shape
    H, R = HEADS, D // HEADS
    P = 128
    T = S // P
    F = k0.shape[1]
    FT = F // P
    SCALE = float(R) ** -0.5
    G = 4
    STEPS = 10
    HALF = H // 2
    MAX_RING = 3
    QK_ROWS, MAX_ROW = 96, 96
    ALL_ROWS = MAX_ROW + 3
    FIRST, LAST = -2, B + 1
    LOOP = (3, B - 3)
    assert (D, H, T, FT, R) == (128, 16, 4, 4, 8) and (LOOP[1] - LOOP[0]) % UNROLL == 0

    def live(b):
        return b.reg is not None or 0 <= b.c < B

    USES = len(BANK_USES)
    used_before = {FIRST: 0}
    for n in range(FIRST, LAST + 1):
        used_before[n + 1] = used_before[n] + sum(0 <= n + d < B for _, d in BANK_USES)
    assert used_before[LOOP[1]] - used_before[LOOP[0]] == USES * (LOOP[1] - LOOP[0]) and UNROLL % 2 == 0

    def use(n, what):
        before = [d for w, d in BANK_USES[:[w for w, _ in BANK_USES].index(what)]]
        if n.reg is None:
            i = used_before[n.c] + sum(0 <= n.c + d < B for d in before)
            return i % 2, i // 2 + 1
        i = used_before[LOOP[0]] + USES * (n.c - LOOP[0]) + len(before)
        return i % 2, n.reg * (UNROLL * USES // 2) + (i // 2 + 1)

    def use_of(b, what):
        return use(b + -dict(BANK_USES)[what], what)

    with ExitStack() as ctx:
        def sb(name, shape, dt=F32):
            return ctx.enter_context(nc.sbuf_tensor(name, shape, dt))

        def sem(name):
            return ctx.enter_context(nc.semaphore(name))

        score_ps = ctx.enter_context(nc.psum_tensor("score_ps", [P, 2, S], F32))
        max_ps = ctx.enter_context(nc.psum_tensor("max_ps", [P, MAX_RING, S], F32))
        av_ps = ctx.enter_context(nc.psum_tensor("av_ps", [P, S], F32))
        bank_ps = ctx.enter_context(nc.psum_tensor("bank_ps", [P, 2, S], F32))

        ident = sb("ident", [P, P])
        ident_bf = sb("ident_bf", [P, P], BF16)
        future_bf = sb("future_bf", [P, P], BF16)
        mult = sb("mult", [P, T, 3])
        minus_half = sb("minus_half", [P, T])
        one = sb("one", [1, P])
        exp_one = sb("exp_one", [1, 1])
        wc = sb("wc", [P, 3 * D])
        wqk = sb("wqk", [P, 2, P])
        wp = sb("wp", [P, D])
        bqk_row = sb("bqk_row", [1, 3 * D])
        bqk_perm = sb("bqk_perm", [1, 2, P])
        bqk = sb("bqk", [P, 2])
        bv = sb("bv", [P, D])
        bp = sb("bp", [P, D])
        scales = sb("scales", [P, 3])
        scales2 = sb("scales2", [P, 3])
        w0 = sb("w0", [P, F], F32R)
        w1 = sb("w1", [P, FT, F], F32R)
        w2 = sb("w2", [P, FT, D], F32R)

        stack = [sb(f"stack{i}", [P, H, 2, S], BF16) for i in range(2)]
        x_in = sb("x_in", [P, T, D])
        x_res = sb("x_res", [P, T, D])
        xT = sb("xT", [P, S])
        qk = sb("qk", [P, 2, S])
        parts = sb("parts", [P, 6, S], BF16)
        vaug = [sb(f"vaug{i}", [P, T, H, R + 1]) for i in range(2)]
        negmax = sb("negmax", [P, 2, T, HALF])
        negmax_rest = sb("negmax_rest", [P, 2, T, HALF])
        negmax_parts = sb("negmax_parts", [P, 2, T, 3, HALF], BF16)
        negmaxT = sb("negmaxT", [3 * HALF, 2, S], BF16)
        e = [sb(f"e{i}", [P, STEPS, S]) for i in range(2)]
        avT = sb("avT", [P, G, S])
        recip = sb("recip", [P, 2, H])
        attn = sb("attn", [P, T, D])
        attnT = sb("attnT", [P, S])
        res1 = sb("res1", [P, T, D])
        x1 = sb("x1", [P, T, D])
        stats = sb("stats", [P, 2, T, 6])
        moments = sb("moments", [P, 2, T, 2])
        var_eps = sb("var_eps", [P, 2, T])
        rstd = sb("rstd", [P, 2, T])
        neg_mean = sb("neg_mean", [P, 2, T])
        shift = sb("shift", [P, 2, T])
        full = sb("full", [P, 2, S])
        x1_hi = sb("x1_hi", [P, S], F32R)
        x1_lo = sb("x1_lo", [P, S], F32R)
        h_hi = [sb(f"h{i}_hi", [P, FT, S], F32R) for i in range(2)]
        h_lo = [sb(f"h{i}_lo", [P, FT, S], F32R) for i in range(2)]
        res2 = sb("res2", [P, T, D])

        raw0 = e[0][:, 0:2, :].rearrange("p a s -> p (a s)").bitcast(mybir.dt.uint8)[:, 0:2 * F]
        raw1 = e[0][:, 2:4, :].rearrange("p a s -> p (a s)").bitcast(mybir.dt.uint8)[:, 0:FT * F]
        raw2 = e[0][:, 4:5, :].rearrange("p a s -> p (a s)").bitcast(mybir.dt.uint8)[:, 0:FT * D]
        w0_half = e[0][:, 5, :]

        w_loaded = sem("w_loaded")
        ffn_loaded = sem("ffn_loaded")
        consts_step = sem("consts_step")
        consts_ready = sem("consts_ready")
        stack_cleared = [sem(f"stack{i}_cleared") for i in range(2)]
        setup_step = sem("setup_step")
        bias_row = sem("bias_row")
        x_loaded = sem("x_loaded")
        xres_loaded = sem("xres_loaded")
        xres_biased = sem("xres_biased")
        bank_full = [sem(f"bank{i}_full") for i in range(2)]
        bank_free = [sem(f"bank{i}_free") for i in range(2)]
        split_step = sem("split_step")
        stacked = [sem(f"stacked{i}") for i in range(2)]
        v_ready = sem("v_ready")
        max_scored = sem("max_scored")
        max_taken = sem("max_taken")
        negmax_step = sem("negmax_step")
        negmax_in = [sem(f"negmax_in{i}") for i in range(2)]
        scored = sem("scored")
        exped = sem("exped")
        masked = sem("masked")
        summed = sem("summed")
        av_out = sem("av_out")
        recip_ready = sem("recip_ready")
        ln_step = [sem(f"ln{i + 1}_step") for i in range(2)]
        rstd_ready = [sem(f"rstd{i + 1}_ready") for i in range(2)]
        hi_ready = sem("hi_ready")
        split_ready = sem("split_ready")
        stored = sem("stored")

        x_tok = x.rearrange("b (t p) d -> b p t d", p=P)
        out_tok = out.rearrange("b (t p) d -> b p t d", p=P)

        block = ctx.enter_context(nc.Block())

        def run(eng, iteration):
            for n in range(FIRST, LOOP[0]):
                iteration(At(n))
            with eng.Fori(0, (LOOP[1] - LOOP[0]) // UNROLL) as i:
                for u in range(UNROLL):
                    iteration(At(LOOP[0] + u, i))
            for n in range(LOOP[1], LAST + 1):
                iteration(At(n))

        def wait_full(eng, u):
            eng.wait_ge(bank_full[u[0]], u[1])

        def wait_free(eng, u):
            eng.wait_ge(bank_free[u[0]], u[1])

        def apart(eng):
            eng.nop(nofuse=True)

        def last_batch(b):
            return b.reg is None and b.c == B - 1

        def full_slot(b, k):
            return (b.c * 9 + k) % 2

        @block.sync
        def _(sp):
            sp.dma_start(x_in[:], x_tok[0]).then_inc(x_loaded, 16)
            sp.dma_start(wc[:], w_qkv).then_inc(w_loaded, 16)
            sp.dma_start(bqk_row[:], b_qkv.rearrange("(a n) -> a n", a=1)).then_inc(w_loaded, 16)
            sp.dma_start(bv[:], b_qkv[2 * D:3 * D].partition_broadcast(P)).then_inc(w_loaded, 16)
            sp.dma_start(bp[:], b_proj.partition_broadcast(P)).then_inc(w_loaded, 16)
            sp.dma_start(wp[:], w_proj).then_inc(w_loaded, 16)
            sp.dma_start(raw0.rearrange("p (a n) -> p a n", a=2),
                         k0.rearrange("(a p) n -> p a n", p=P)).then_inc(ffn_loaded, 16)
            sp.dma_start(raw1.rearrange("p (a n) -> p a n", a=FT),
                         k1.rearrange("(a p) n -> p a n", p=P)).then_inc(ffn_loaded, 16)
            sp.dma_start(raw2.rearrange("p (a n) -> p a n", a=FT),
                         k2.rearrange("(a p) n -> p a n", p=P)).then_inc(ffn_loaded, 16)
            for i, s in enumerate((s0, s1, s2)):
                sp.dma_start(scales[:, i:i + 1], s.partition_broadcast(P)).then_inc(ffn_loaded, 16)

            def stack_half(b, half, levels=(0, 1, 2)):
                for a in range(3):
                    for c in range(3):
                        row = R * (3 * a + c)
                        if max(a, c) in levels:
                            src = parts[64 * half:64 * half + 64, c:3 + a + 1:3 + a - c, :]
                            sp.dma_start(stack[b.parity][row:row + R, HALF * half:HALF * half + HALF, :, :],
                                         src).then_inc(stacked[half], 16)

            def store(b):
                sp.wait_ge(ln_step[1], b.times(4, 4))
                sp.dma_start(out_tok[b.times(1)], res2[:]).then_inc(stored, 16)

            def negmax_rows(b, half):
                wait_free(sp, use_of(b, f"negmax{half}"))
                sp.dma_start(stack[b.parity][MAX_ROW:ALL_ROWS, HALF * half:HALF * half + HALF, 0, :],
                             negmaxT[:, half, :]).then_inc(negmax_in[half], 16)

            def iteration(n):
                b = n + 2
                if live(b) and not (b.reg is None and b.c == 0):
                    wait_full(sp, use_of(b + -1, "xT"))
                    sp.dma_start(x_in[:], x_tok[b.times(1)]).then_inc(x_loaded, 16)
                b = n + -1
                if live(b):
                    if b.c > 0 or b.reg is not None:
                        wait_free(sp, use_of(b + -1, "proj"))
                    sp.dma_start(x_res[:], x_tok[b.times(1)]).then_inc(xres_loaded, 16)
                if live(n):
                    negmax_rows(n, 1)
                if live(n + 1):
                    negmax_rows(n + 1, 0)
                b = n + 2
                if b.reg is None and b.c == 0:
                    wait_free(sp, use_of(b, "q"))
                    wait_free(sp, use_of(b, "k"))
                    for half in range(2):
                        stack_half(b, half, levels=(0,))
                    sp.wait_ge(split_step, 2)
                    stack_half(b, 0, levels=(1,))
                    sp.wait_ge(split_step, 3)
                    sp.wait_ge(stack_cleared[0], 2)
                    stack_half(b, 0, levels=(2,))
                    stack_half(b, 1, levels=(1, 2))
                elif live(b):
                    sp.wait_ge(split_step, b.times(3, 3))
                    apart(sp)
                    if live(n):
                        sp.wait_ge(scored, n.times(G * STEPS, 2 * STEPS))
                    else:
                        sp.wait_ge(stack_cleared[b.parity], 2)
                    stack_half(b, 0)
                if live(n + -2):
                    store(n + -2)
                if live(b) and not (b.reg is None and b.c == 0):
                    if live(n):
                        sp.wait_ge(scored, n.times(G * STEPS, 4 * STEPS))
                    stack_half(b, 1)

            run(sp, iteration)
            sp.wait_ge(stored, 16 * B)

        @block.gpsimd
        def _(pool):
            step = 0
            for t, v in ((ident, 0.0), (ident_bf, 0.0), (future_bf, 0.0), (mult, FOCUS)):
                nc.gpsimd.memset(t[:], v).then_inc(consts_step, 1)
                step += 1
            nc.gpsimd.memset(minus_half[:], -0.5).then_inc(consts_step, 1)
            nc.gpsimd.memset(one[:], 1.0).then_inc(consts_step, 1)
            step += 2
            pool.wait_ge(consts_step, step)
            for t in (ident, ident_bf):
                nc.gpsimd.affine_select(out=t[:], in_=t[:], compare_op=ALU.not_equal, fill=1.0, base=0,
                                        pattern=[[-1, P]], channel_multiplier=1).then_inc(consts_step, 1)
            nc.gpsimd.affine_select(out=future_bf[:], in_=future_bf[:], compare_op=ALU.is_ge, fill=NEG, base=0,
                                    pattern=[[1, P]], channel_multiplier=-1).then_inc(consts_step, 1)
            first_end = max(1, S // 3)
            second_end = max(first_end + 1, 2 * S // 3)
            step += 3
            for h, base, sign in ((0, first_end - 1, -1), (1, -first_end, 1), (2, -second_end, 1),
                                  (1, second_end - 1, -1)):
                pool.wait_ge(consts_step, step)
                nc.gpsimd.affine_select(out=mult[:, :, h:h + 1], in_=mult[:, :, h:h + 1], compare_op=ALU.is_ge,
                                        fill=1.0, base=base, pattern=[[sign * P, T], [0, 1]],
                                        channel_multiplier=sign).then_inc(consts_step, 1)
                step += 1
            pool.wait_ge(consts_step, step)
            nc.gpsimd.memset(recip[:], 1.0).then_inc(consts_ready, 1)
            pool.wait_ge(consts_ready, 1)

            for i in range(2):
                nc.gpsimd.memset(stack[i][64:P].rearrange("p h a s -> p (h a s)").bitcast(F32),
                                 0.0).then_inc(stack_cleared[i], 1)
                pool.wait_ge(stack_cleared[i], 1)
                nc.gpsimd.memset(stack[i][MAX_ROW:P, :, 1, :].bitcast(F32), TWO_ONES).then_inc(stack_cleared[i], 1)
                pool.wait_ge(stack_cleared[i], 2)

            def split(b, k):
                if k == 0:
                    wait_free(pool, use_of(b, "q"))
                    wait_free(pool, use_of(b, "k"))
                else:
                    pool.wait_ge(split_step, b.times(3, k))
                if k == 0:
                    ins = nc.gpsimd.tensor_tensor(qk[:], qk[:], parts[:, 0:4:3, :], ALU.subtract)
                else:
                    ins = nc.gpsimd.tensor_tensor(parts[:, 2:6:3, :], qk[:], parts[:, 1:5:3, :], ALU.subtract)
                ins.then_inc(split_step, 1)

            def mask(n, g, k):
                buf = e[g % 2]
                if k == 0:
                    after, blocks = 4, (buf[:, 0:4, 0:P],)
                elif k == 1:
                    after, blocks = 8, (buf[:, 4:8, 0:P], buf[:, 4:8, 3 * P:S])
                else:
                    halves = buf[:, 8:10, :].rearrange("p h (a c) -> p (h a) c", c=2 * P)
                    after, blocks = 10, (halves[:, :, 0:P],)
                pool.wait_ge(exped, n.times(G * STEPS, STEPS * g + after))
                apart(pool)
                for ap in blocks:
                    last = nc.gpsimd.affine_select(out=ap, in_=ap, compare_op=ALU.is_ge, fill=0.0, base=0,
                                                   pattern=[[0, 4], [1, P]], channel_multiplier=-1)
                last.then_inc(masked, 1)

            def low_part(b, layer, m):
                k = 1 + FT * layer + m
                pool.wait_ge(hi_ready, b.times(9, k + 1))
                nc.gpsimd.tensor_tensor(h_lo[layer][:, m, :], full[:, full_slot(b, k), :],
                                        h_hi[layer][:, m, :].bitcast(F32), ALU.subtract).then_inc(split_ready, 1)

            def rstd_of(b, i):
                pool.wait_ge(ln_step[i], b.times(4, 3))
                nc.gpsimd.tensor_tensor(rstd[:, i, :], var_eps[:, i, :], minus_half[:],
                                        ALU.pow).then_inc(rstd_ready[i], 1)
                pool.wait_ge(rstd_ready[i], b.times(2, 1))
                nc.gpsimd.tensor_tensor(shift[:, i, :], neg_mean[:, i, :], rstd[:, i, :],
                                        ALU.mult).then_inc(rstd_ready[i], 1)

            def iteration(n):
                def low(layer, m):
                    b = n + (-2 if layer else -1)
                    if live(b) and not last_batch(b):
                        low_part(b, layer, m)

                def bias_residual():
                    b = n + -1
                    if live(b):
                        pool.wait_ge(xres_loaded, b.times(16, 16))
                        nc.gpsimd.tensor_tensor(x_res[:], x_res[:], bp[:].unsqueeze(1).broadcast_to([P, T, D]),
                                                ALU.add).then_inc(xres_biased, 1)

                def split_qk(k):
                    b = n + 2
                    if live(b) and not (b.reg is None and b.c == 0):
                        split(b, k)

                def rstd_of_layer(i):
                    b = n + (-2 if i else -1)
                    if live(b):
                        rstd_of(b, i)

                def masks(g, k):
                    if live(n):
                        mask(n, g, k)

                masks(0, 0)
                low(1, 0)
                low(1, 1)
                masks(0, 1)
                low(1, 2)
                masks(0, 2)
                low(1, 3)
                masks(1, 0)
                bias_residual()
                masks(1, 1)
                split_qk(0)
                masks(1, 2)
                rstd_of_layer(1)
                split_qk(2)
                masks(2, 0)
                rstd_of_layer(0)
                masks(2, 1)
                masks(2, 2)
                masks(3, 0)
                low(0, 0)
                low(0, 1)
                masks(3, 1)
                low(0, 2)
                low(0, 3)
                masks(3, 2)

            pool.wait_ge(w_loaded, 16 * 5)
            run(pool, iteration)

        @block.scalar
        def _(act):
            act.wait_ge(consts_ready, 1)
            nc.scalar.activation(exp_one[:], one[0:1, 0:1], ACT.Exp)
            act.wait_ge(setup_step, 6)

            def take(u, out_ap, func, **kw):
                wait_full(act, u)
                nc.scalar.activation(out_ap, bank_ps[:, u[0], :], func, **kw).then_inc(bank_free[u[0]], 1)

            def exp(n, g, t):
                act.wait_ge(scored, n.times(G * STEPS, STEPS * g + t + 1))
                if n.reg is None and n.c == 0 and g == 0 and t == 0:
                    act.wait_ge(setup_step, 9)
                if t == 0 and not (n.reg is None and n.c * G + g < 2):
                    act.wait_ge(summed, n.times(G, g - 1))
                nc.scalar.activation(e[g % 2][:, t, :], score_ps[:, t % 2, :], ACT.Exp,
                                     scale=SCALE).then_inc(exped, 1)

            def sums_out(b, g):
                act.wait_ge(summed, b.times(G, g + 1))
                if g == 0 and (b.reg is not None or b.c > 0):
                    wait_full(act, use_of(b + -1, "tok_3"))
                nc.scalar.activation(avT[:, g, :], av_ps[:], ACT.Copy).then_inc(av_out, 1)

            def activation_out(b, k, what, func, **kw):
                if b.reg is not None or b.c * 9 + k >= 2:
                    act.wait_ge(split_ready, b.times(9, k - 1))
                take(use_of(b, what), full[:, full_slot(b, k), :], func, **kw)

            def layernorm_out(b, i, t, src, dst):
                if t == 0:
                    act.wait_ge(rstd_ready[i], b.times(2, 2))
                ins = nc.scalar.activation(dst[:, t, :], src[:, t, :], ACT.Identity,
                                           scale=rstd[:, i, t:t + 1], bias=shift[:, i, t:t + 1])
                if t == T - 1:
                    ins.then_inc(ln_step[i], 1)

            def iteration(n):
                for g in range(G):
                    for t in range(STEPS):
                        if live(n):
                            exp(n, g, t)
                        for i in range(T):
                            if (g, t) == LN_OUT[0][i] and live(n + -1):
                                layernorm_out(n + -1, 0, i, res1, x1)
                            if (g, t) == LN_OUT[1][i] and live(n + -2):
                                layernorm_out(n + -2, 1, i, res2, res2)
                        if t == SUMS_OUT:
                            if g == 0 and live(n + -1):
                                sums_out(n + -1, 3)
                            if g > 0 and live(n):
                                sums_out(n, g - 1)
                        for what, d, _, step in PLACES:
                            b = n + d
                            if step != (g, t) or not live(b):
                                continue
                            if what[:4] == "ffn1":
                                activation_out(b, 5 + int(what[5]), what, ACT.Relu, scale=scales2[:, 1:2])
                            if what == "xT":
                                if live(n + 1):
                                    wait_full(act, use_of(n + 1, "v"))
                                take(use_of(b, what), xT[:], ACT.Copy)
                            if what in ("q", "k"):
                                i = "qk".index(what)
                                if i == 0 and (b.reg is not None or b.c > 0):
                                    for half in range(2):
                                        act.wait_ge(stacked[half], b.times(9 * 16))
                                u = use_of(b, what)
                                wait_full(act, u)
                                nc.scalar.activation(parts[:, 3 * i, :], bank_ps[:, u[0], :], ACT.Identity,
                                                     bias=bqk[:, i:i + 1])
                                take(u, qk[:, i, :], ACT.Identity, bias=bqk[:, i:i + 1])
                            if what == "ffn2T":
                                take(use_of(b, what), attnT[:], ACT.Identity, scale=scales2[:, 2:3])
                            if what == "attnT":
                                take(use_of(b, what), attnT[:], ACT.Copy)
                            if what == "x1T":
                                activation_out(b, 0, what, ACT.Copy)
                            if what[:4] == "ffn0":
                                activation_out(b, 1 + int(what[5]), what, ACT.Relu, scale=scales[:, 0:1])
                        if (g, t) == MIDDLE_STEP and live(n + 2):
                            act.wait_ge(split_step, (n + 2).times(3, 1))
                            nc.scalar.activation(parts[:, 1:5:3, :], qk[:], ACT.Copy).then_inc(split_step, 1)

            run(act, iteration)

        @block.vector
        def _(dve):
            nc.vector.memset(av_ps[:], 0.0).then_inc(setup_step, 1)
            for i in range(2):
                nc.vector.memset(vaug[i][:, :, :, R:R + 1], 1.0).then_inc(setup_step, 1)
            dve.wait_ge(w_loaded, 16 * 5)
            for i in range(2):
                for half in range(2):
                    cols = slice(D * i + 64 * half, D * i + 64 * half + 64)
                    ws = wc[:, cols].rearrange("p (h r) -> p r h", r=R)
                    bs = bqk_row[:, cols].rearrange("p (h r) -> p r h", r=R)
                    nc.vector.tensor_copy(
                        wqk[:, i, 64 * half:64 * half + 64].rearrange("p (r h) -> p r h", r=R), ws)
                    last = nc.vector.tensor_copy(
                        bqk_perm[:, i, 64 * half:64 * half + 64].rearrange("p (r h) -> p r h", r=R), bs)
            last.then_inc(setup_step, 1)
            dve.wait_ge(consts_ready, 1)
            dve.wait_ge(setup_step, 4)
            for i in range(2):
                last = nc.vector.tensor_copy(vaug[i][:, :, 0:3, R:R + 1], mult[:].unsqueeze(3))
            last.then_inc(setup_step, 1)
            dve.wait_ge(bias_row, 1)
            nc.vector.tensor_copy(bqk[:], max_ps[:, 0, 0:2]).then_inc(setup_step, 1)
            dve.wait_ge(ffn_loaded, 16 * 6)
            nc.vector.tensor_scalar(scales2[:], scales[:], 2.0, None, ALU.mult).then_inc(setup_step, 1)
            nc.vector.tensor_scalar(w0_half, raw0[:, F:2 * F], -2.0, None, ALU.mult).then_inc(setup_step, 1)
            dve.wait_ge(setup_step, 8)
            nc.vector.scalar_tensor_tensor(w0[:], raw0[:, 0:F], 2.0, w0_half, ALU.mult, ALU.add)
            nc.vector.tensor_scalar(w1[:].rearrange("p a n -> p (a n)"), raw1, 2.0, -1.0, ALU.mult, ALU.add)
            nc.vector.tensor_scalar(w2[:].rearrange("p a n -> p (a n)"), raw2, 2.0, -1.0, ALU.mult,
                                    ALU.add).then_inc(setup_step, 1)
            wait_free(dve, use_of(At(0), "q"))
            wait_free(dve, use_of(At(0), "k"))
            nc.vector.tensor_tensor(qk[:], qk[:], parts[:, 0:4:3, :], ALU.subtract).then_inc(split_step, 1)
            dve.wait_ge(split_step, 2)
            nc.vector.tensor_tensor(parts[:, 2:6:3, :], qk[:], parts[:, 1:5:3, :],
                                    ALU.subtract).then_inc(split_step, 1)

            def take_max(b, g, t):
                buf = max_ps[:, (STEPS * g + t) % MAX_RING, :]
                half, h = g // 2, G * (g % 2)
                dve.wait_ge(max_scored, b.times(G * STEPS, STEPS * g + t + 1))
                if t < 4:
                    ins = nc.vector.reduce_max(negmax[:, half, 3, h + t:h + t + 1], buf, AX.X, negate=True)
                elif t < 8:
                    i = h + t - 4
                    nc.vector.reduce_max(negmax[:, half, 2, i:i + 1], buf[:, 0:3 * P], AX.X, negate=True)
                    ins = nc.vector.reduce_max(negmax[:, half, 0, i:i + 1], buf[:, 3 * P:S], AX.X, negate=True)
                else:
                    i = h + 2 * (t - 8)
                    ins = nc.vector.reduce_max(negmax[:, half, 1, i:i + 2],
                                               buf.rearrange("p (h k) -> p h k", h=2), AX.X, negate=True)
                ins.then_inc(max_taken, 1)

            def split_negmax(b, half, k):
                m, r = negmax[:, half], negmax_rest[:, half]
                hi, mid, lo = (negmax_parts[:, half, :, i, :] for i in range(3))
                if k:
                    dve.wait_ge(negmax_step, b.times(8, 4 * half + k))
                else:
                    dve.wait_ge(max_taken, b.times(G * STEPS, 2 * STEPS * (half + 1)))
                if k == 0:
                    ins = nc.vector.tensor_copy(hi, m)
                elif k == 1:
                    ins = nc.vector.tensor_tensor(r, m, hi, ALU.subtract)
                elif k == 2:
                    ins = nc.vector.tensor_copy(mid, r)
                else:
                    ins = nc.vector.tensor_tensor(lo, r, mid, ALU.subtract)
                ins.then_inc(negmax_step, 1)

            def take_negmaxT(b, half):
                u = use_of(b, f"negmax{half}")
                wait_full(dve, u)
                if b.reg is not None or b.c > 0:
                    dve.wait_ge(negmax_in[half], b.times(16))
                src = bank_ps[0:3 * HALF, u[0], :].bitcast(BF16)[:, 0:S]
                nc.vector.tensor_copy(negmaxT[:, half, :], src).then_inc(bank_free[u[0]], 1)

            def take_v(b):
                u = use_of(b, "v")
                wait_full(dve, u)
                va = vaug[b.parity]
                if b.reg is not None or b.c > 1:
                    dve.wait_ge(summed, b.times(G, -G))
                nc.vector.tensor_tensor(va[:, :, :, 0:R], bank_ps[:, u[0], :].rearrange("p (t h r) -> p t h r", t=T, r=R),
                                        bv[:].rearrange("p (h r) -> p h r", r=R).unsqueeze(1).broadcast_to([P, T, H, R]),
                                        ALU.add).then_inc(bank_free[u[0]], 1)
                wait_free(dve, u)
                nc.vector.tensor_tensor(va[:, :, 0:3, 0:R], va[:, :, 0:3, 0:R],
                                        mult[:].unsqueeze(3).broadcast_to([P, T, 3, R]), ALU.mult).then_inc(v_ready, 1)

            def normalise(b, t):
                u = use_of(b, f"tok_{t}")
                wait_full(dve, u)
                src = bank_ps[:, u[0], :].rearrange("p (h c) -> p h c", c=32)
                nc.vector.reciprocal(recip[:, t % 2, :].unsqueeze(2), src[:, :, R:R + 1]).then_inc(recip_ready, 1)
                dve.wait_ge(recip_ready, b.times(T, t + 1))
                nc.vector.tensor_tensor(attn[:, t, :].rearrange("p (h r) -> p h r", r=R), src[:, :, 0:R],
                                        recip[:, t % 2, :].unsqueeze(2).broadcast_to([P, H, R]),
                                        ALU.mult).then_inc(bank_free[u[0]], 1)

            def layernorm_stats(i, src, u):
                wait_free(dve, u)
                for t in range(T):
                    ins = nc.vector.bn_stats(stats[:, i, t, :], src[:, t, :])
                ins.then_inc(ln_step[i], 1)

            def layernorm_var(b, i):
                dve.wait_ge(ln_step[i], b.times(4, 1))
                apart(dve)
                for t in range(T):
                    ins = nc.vector.bn_aggr(moments[:, i, t, :], stats[:, i, t, :])
                ins.then_inc(ln_step[i], 1)
                dve.wait_ge(ln_step[i], b.times(4, 2))
                nc.vector.tensor_scalar(neg_mean[:, i, :].unsqueeze(2), moments[:, i, :, 0:1], -1.0, None, ALU.mult)
                nc.vector.tensor_scalar(var_eps[:, i, :].unsqueeze(2), moments[:, i, :, 1:2], EPS, None,
                                        ALU.add).then_inc(ln_step[i], 1)

            def high_part(b, k, hi, what):
                wait_free(dve, use_of(b, what))
                nc.vector.tensor_copy(hi, full[:, full_slot(b, k), :]).then_inc(hi_ready, 1)

            def low_part(b, k, hi, lo):
                dve.wait_ge(hi_ready, b.times(9, k + 1))
                nc.vector.tensor_tensor(lo, full[:, full_slot(b, k), :], hi.bitcast(F32),
                                        ALU.subtract).then_inc(split_ready, 1)

            def iteration(n):
                for g in range(G):
                    for t in range(STEPS):
                        if live(n + 1):
                            take_max(n + 1, g, t)
                        for what, d, _, step in PLACES:
                            b = n + d
                            if step != (g, t) or not live(b):
                                continue
                            if what[:6] == "negmax":
                                take_negmaxT(b, int(what[6]))
                            if what == "v":
                                take_v(b)
                            if what[:3] == "tok":
                                normalise(b, int(what[4]))
                            if what == "ffn2":
                                u = use_of(b, what)
                                wait_full(dve, u)
                                if b.reg is not None or b.c > 0:
                                    dve.wait_ge(stored, b.times(16))
                                nc.vector.tensor_tensor(
                                    res2[:].rearrange("p t d -> p (t d)"), bank_ps[:, u[0], :],
                                    x1[:].rearrange("p t d -> p (t d)"), ALU.add).then_inc(bank_free[u[0]], 1)
                                layernorm_stats(1, res2, u)
                            if what == "proj":
                                u = use_of(b, what)
                                wait_full(dve, u)
                                dve.wait_ge(xres_biased, b.times(1, 1))
                                nc.vector.tensor_tensor(res1[:].rearrange("p t d -> p (t d)"), bank_ps[:, u[0], :],
                                                        x_res[:].rearrange("p t d -> p (t d)"),
                                                        ALU.add).then_inc(bank_free[u[0]], 1)
                                layernorm_stats(0, res1, u)
                        for what, step in HIGH_STEPS.items():
                            b = n + dict(BANK_USES)[what]
                            if step != (g, t) or not live(b):
                                continue
                            if what == "x1T":
                                high_part(b, 0, x1_hi[:], what)
                                low_part(b, 0, x1_hi[:], x1_lo[:])
                            else:
                                layer, m = int(what[3]), int(what[5])
                                k = 1 + FT * layer + m
                                high_part(b, k, h_hi[layer][:, m, :], what)
                                if last_batch(b):
                                    low_part(b, k, h_hi[layer][:, m, :], h_lo[layer][:, m, :])
                        for k in range(4):
                            if (g, t) == NEGMAX_SPLIT[0][k] and live(n + 1):
                                split_negmax(n + 1, 0, k)
                            if (g, t) == NEGMAX_SPLIT[1][k] and live(n):
                                split_negmax(n, 1, k)
                        if (g, t) == LN_VAR[0] and live(n + -1):
                            layernorm_var(n + -1, 0)
                        if (g, t) == LN_VAR[1] and live(n + -2):
                            layernorm_var(n + -2, 1)

            run(dve, iteration)

        @block.tensor
        def _(pe):
            pe.wait_ge(setup_step, 4)
            pe.wait_ge(consts_ready, 1)
            for i in range(2):
                last = nc.tensor.matmul(max_ps[:, 0, i:i + 1], bqk_perm[0:1, i, :], one[0:1, 0:1],
                                        start=(i == 0), stop=True, skip_group_check=True)
            last.then_inc(bias_row, 1)
            pe.wait_ge(setup_step, 6)

            def claim(u):
                if not (isinstance(u[1], int) and u[1] == 1):
                    pe.wait_ge(bank_free[u[0]], u[1] + -1)
                return bank_ps[:, u[0], :]

            def transposes(u, sources, into=None):
                bank = claim(u)
                for i, src in enumerate(sources):
                    last = nc.tensor.transpose(bank[:, P * i:P * i + P], src, ident[:])
                last.then_inc(bank_full[u[0]], 1)

            def max_scores(b, g, t):
                i = STEPS * g + t
                st, out_ap = stack[b.parity], max_ps[:, i % MAX_RING, :]
                if t == 0 and g % 2 == 0:
                    pe.wait_ge(stacked[g // 2], b.times(9 * 16, 9 * 16))
                last_use = i - MAX_RING
                if i < MAX_RING:
                    last_use = max(j - G * STEPS for j in range(G * STEPS) if j % MAX_RING == i)
                if not (b.reg is None and b.c == 0 and last_use < 0):
                    pe.wait_ge(max_taken, b.times(G * STEPS, last_use + 1))

                def part(h, qt, col):
                    width = P * (qt + 1)
                    nc.tensor.matmul(out_ap[:, col:col + width], st[0:QK_ROWS, h, 0, P * qt:P * qt + P],
                                     st[0:QK_ROWS, h, 1, 0:width], start=True, stop=False)
                    return nc.tensor.matmul(out_ap[:, col + width - P:col + width], future_bf[:], ident_bf[:],
                                            start=False, stop=True)
                if t < 4:
                    last = part(G * g + t, 3, 0)
                elif t < 8:
                    part(G * g + t - 4, 2, 0)
                    last = part(G * g + t - 4, 0, 3 * P)
                else:
                    part(G * g + 2 * (t - 8), 1, 0)
                    last = part(G * g + 2 * (t - 8) + 1, 1, 2 * P)
                last.then_inc(max_scored, 1)

            def scores(n, g, t):
                st, out_ap = stack[n.parity], score_ps[:, t % 2, :]
                if t == 0 and g % 2 == 0:
                    pe.wait_ge(negmax_in[g // 2], n.times(16, 16))
                if not (n.reg is None and n.c == 0 and g == 0 and t < 2):
                    pe.wait_ge(exped, n.times(G * STEPS, STEPS * g + t - 1))

                def part(h, kt, col):
                    width = S - P * kt
                    return nc.tensor.matmul(out_ap[:, col:col + width], st[0:ALL_ROWS, h, 1, P * kt:P * kt + P],
                                            st[0:ALL_ROWS, h, 0, P * kt:S], start=True, stop=True)
                if t < 4:
                    last = part(G * g + t, 0, 0)
                elif t < 8:
                    part(G * g + t - 4, 1, 0)
                    last = part(G * g + t - 4, 3, 3 * P)
                else:
                    part(G * g + 2 * (t - 8), 2, 0)
                    last = part(G * g + 2 * (t - 8) + 1, 2, 2 * P)
                last.then_inc(scored, 1)

            def sums(b, g, kt, order):
                if order == 0:
                    pe.wait_ge(masked, b.times(3 * G, 3 * g + 1))
                    if g == 0:
                        pe.wait_ge(v_ready, b.times(1, 1))
                    if not (b.reg is None and b.c == 0 and g == 0):
                        pe.wait_ge(av_out, b.times(G, g))
                elif order == 1:
                    pe.wait_ge(masked, b.times(3 * G, 3 * g + 2))
                elif order == 3:
                    pe.wait_ge(masked, b.times(3 * G, 3 * g + 3))
                for j in range(G):
                    if kt == 0:
                        src = e[g % 2][:, j, :]
                    elif kt == 1:
                        src = e[g % 2][:, 4 + j, 0:3 * P]
                    elif kt == 3:
                        src = e[g % 2][:, 4 + j, 3 * P:S]
                    else:
                        src = e[g % 2][:, 8 + j // 2, 2 * P * (j % 2):2 * P * (j % 2) + 2 * P]
                    last = nc.tensor.matmul(av_ps[32 * j:32 * j + R + 1, P * kt:S],
                                            vaug[b.parity][:, kt, G * g + j, :], src,
                                            start=(order == 0), stop=(order == 3))
                if order == 3:
                    last.then_inc(summed, 1)

            def negmax_transposes(b, half):
                u = use_of(b, f"negmax{half}")
                pe.wait_ge(negmax_step, b.times(8, 4 * half + 4))
                bank = claim(u).bitcast(BF16)
                for qt in range(T):
                    last = nc.tensor.transpose(bank[0:3 * HALF, P * qt:P * qt + P],
                                               negmax_parts[:, half, qt].rearrange("p c h -> p (c h)"), ident_bf[:])
                last.then_inc(bank_full[u[0]], 1)

            def token_transposes(b, t):
                if t == 0:
                    pe.wait_ge(av_out, b.times(G, G))
                transposes(use_of(b, f"tok_{t}"), [avT[:, g, P * t:P * t + P] for g in range(G)])

            def ffn(b, what, pairs, splits=()):
                u = use_of(b, what)
                bank = claim(u)
                for i, (w, hi, lo) in enumerate(pairs):
                    if splits:
                        pe.wait_ge(split_ready, b.times(9, splits[i]))
                    nc.tensor.matmul(bank, w, hi, start=(i == 0), stop=False)
                    last = nc.tensor.matmul(bank, w, lo, start=False, stop=(i == len(pairs) - 1))
                last.then_inc(bank_full[u[0]], 1)

            def fill(n, g, t):
                b = n + -2
                for k in range(FT):
                    if (g, t) != FFN2_STEPS[k] or not live(b):
                        continue
                    u = use_of(b, "ffn2T")
                    pe.wait_ge(split_ready, b.times(9, 6 + k))
                    if k == 0:
                        claim(u)
                    bank = bank_ps[:, u[0], :]
                    nc.tensor.matmul(bank, w2[:, k, :], h_hi[1][:, k, :], start=(k == 0), stop=False)
                    last = nc.tensor.matmul(bank, w2[:, k, :], h_lo[1][:, k, :], start=False, stop=(k == FT - 1))
                    if k == FT - 1:
                        last.then_inc(bank_full[u[0]], 1)
                for what, d, step, _ in PLACES:
                    if what != "ffn2T" and step == (g, t) and live(n + d):
                        fill_bank(n + d, what)

            def fill_bank(b, what):
                u = use_of(b, what)
                if what[:6] == "negmax":
                    negmax_transposes(b, int(what[6]))
                if what[:4] == "ffn1":
                    m = int(what[5])
                    ffn(b, what, [(w1[:, k, P * m:P * m + P], h_hi[0][:, k, :], h_lo[0][:, k, :])
                                  for k in range(FT)], splits=(2, 3, 4, 5) if m == 0 else ())
                if what == "v":
                    bank = claim(u)
                    wait_free(pe, use_of(b, "xT"))
                    for kt in range(T):
                        last = nc.tensor.matmul(bank[:, P * kt:P * kt + P], xT[:, P * kt:P * kt + P],
                                                wc[:, 2 * D:3 * D], start=True, stop=True)
                    last.then_inc(bank_full[u[0]], 1)
                if what == "xT":
                    pe.wait_ge(x_loaded, b.times(16, 16))
                    transposes(u, [x_in[:, i, :] for i in range(T)])
                if what[:3] == "tok":
                    token_transposes(b, int(what[4]))
                if what in ("q", "k"):
                    bank = claim(u)
                    wait_free(pe, use_of(b, "xT"))
                    nc.tensor.matmul(bank, wqk[:, "qk".index(what), :], xT[:],
                                     start=True, stop=True).then_inc(bank_full[u[0]], 1)
                if what == "ffn2":
                    wait_free(pe, use_of(b, "ffn2T"))
                    transposes(u, [attnT[:, P * i:P * i + P] for i in range(T)])
                if what == "attnT":
                    wait_free(pe, use_of(b, "tok_3"))
                    transposes(u, [attn[:, i, :] for i in range(T)])
                if what == "proj":
                    bank = claim(u)
                    wait_free(pe, use_of(b, "attnT"))
                    for i in range(T):
                        last = nc.tensor.matmul(bank[:, P * i:P * i + P], attnT[:, P * i:P * i + P], wp[:],
                                                start=True, stop=True)
                    last.then_inc(bank_full[u[0]], 1)
                if what == "x1T":
                    pe.wait_ge(ln_step[0], b.times(4, 4))
                    transposes(u, [x1[:, i, :] for i in range(T)])
                if what[:4] == "ffn0":
                    m = int(what[5])
                    if m == 0 and b.reg is None and b.c == 0:
                        pe.wait_ge(setup_step, 9)
                    ffn(b, what, [(w0[:, P * m:P * m + P], x1_hi[:], x1_lo[:])], splits=(1,) if m == 0 else ())

            def iteration(n):
                for g in range(G):
                    for t in range(STEPS):
                        if live(n + 1):
                            max_scores(n + 1, g, t)
                        if live(n):
                            scores(n, g, t)
                        if t in SUM_STEPS:
                            order = SUM_STEPS.index(t)
                            kt = (0, 1, 3, 2)[order]
                            if g == 0 and live(n + -1):
                                sums(n + -1, 3, kt, order)
                            if g > 0 and live(n):
                                sums(n, g - 1, kt, order)
                        fill(n, g, t)

            run(pe, iteration)


_INS = ["L0_attn_hidden_states", "L0_attn_c_attn_w", "L0_attn_c_attn_b", "L0_attn_c_proj_w", "L0_attn_c_proj_b",
        "L0_ffn_k0", "L0_ffn_k1", "L0_ffn_k2", "L0_ffn_s0", "L0_ffn_s1", "L0_ffn_s2"]


def kernel(**inputs):
    import numpy as _np
    import concourse.bacc as _bacc
    from concourse import mybir as _mybir
    from concourse.bass_utils import run_bass_kernel_spmd as _run

    nc = _bacc.Bacc("TRN2", target_bir_lowering=False, num_devices=1)
    arrays, args = {}, []
    for name in _INS:
        a = _np.ascontiguousarray(inputs[name])
        arrays[f"in_{name}"] = a
        args.append(nc.dram_tensor(f"in_{name}", a.shape, _mybir.dt.from_np(a.dtype), kind="ExternalInput").ap())
    shape = arrays[f"in_{_INS[0]}"].shape
    args.append(nc.dram_tensor("out_x", shape, _mybir.dt.float32, kind="ExternalOutput").ap())
    block_kernel(nc, *args)
    r = _run(nc, [arrays], core_ids=[0])
    return r.results[0]["out_x"]
```
